# Optimizing a Trainium2 kernel written in Bass

```python
import numpy as np
import jax
import jax.numpy as jnp

def _softmax(x, axis=-1):
    return jax.nn.softmax(x, axis=axis)

def _gelu(x):
    return jax.nn.gelu(x, approximate=True)

def _silu(x):
    return jax.nn.silu(x)

def _sigmoid(x):
    return jax.nn.sigmoid(x)

def _layernorm(x, axis=-1, eps=1e-05):
    m = jnp.mean(x, axis=axis, keepdims=True)
    v = jnp.var(x, axis=axis, keepdims=True)
    return (x - m) / jnp.sqrt(v + eps)

def _scatter_add(tgt, idx, src, axis=0):
    return tgt.at[idx].add(src)

def _segment_sum(src, seg, n):
    return jax.ops.segment_sum(src, seg, n)
kernel_name = 'mk_prb_d1_jaxref_r4_515a58'

def setup_inputs(seed: int=0):
    np.random.seed(seed)
    _w = jnp.asarray

    def _L0_attn_setup():
        import jax, jax.numpy as jnp
        import numpy as np
        E2M1_GRID = jnp.array([0.0, 0.5, 1.0, 1.5, 2.0, 3.0, 4.0, 6.0], dtype=jnp.float32)
        E2M1_MIDS = (E2M1_GRID[1:] + E2M1_GRID[:-1]) / 2.0
        FP4_MAX = 6.0
        FP8_E4M3_MAX = 448.0

        def nvfp4_quant_dequant(w):
            O, I = w.shape
            w16 = w.reshape(O, I // 128, 8, 16)
            amax128 = jnp.max(jnp.abs(w16), axis=(-2, -1))
            outer = amax128 / (FP4_MAX * FP8_E4M3_MAX)
            outer = jnp.where(outer > 0, outer, 1.0)
            amax16 = jnp.max(jnp.abs(w16), axis=-1)
            inner = amax16 / FP4_MAX / outer[..., None]
            inner = inner.astype(jnp.float8_e4m3fn).astype(jnp.float32)
            scale = outer[..., None] * inner
            safe = jnp.where(scale > 0, scale, 1.0)[..., None]
            code = w16 / safe
            a = jnp.abs(code)
            idx = jnp.searchsorted(E2M1_MIDS, a)
            q = E2M1_GRID[idx] * jnp.sign(code)
            return (q * scale[..., None]).reshape(O, I)
        key = jax.random.key(seed)
        k0, k1, k2 = jax.random.split(key, 3)
        B, S, H = (2, 512, 512)
        hidden_states = jax.random.normal(k0, (B, S, H), dtype=jnp.float32)
        w_qkv = jax.random.normal(k1, (3 * H, H), dtype=jnp.float32) * 0.023
        w_o = jax.random.normal(k2, (H, H), dtype=jnp.float32) * 0.023
        w_qkv = nvfp4_quant_dequant(w_qkv)
        w_o = nvfp4_quant_dequant(w_o)
        return {'hidden_states': hidden_states, 'w_qkv': w_qkv, 'w_o': w_o}
    _L0_attn_in = _L0_attn_setup()

    def _L0_ffn_setup():
        import jax, jax.numpy as jnp
        import numpy as np
        BLOCK_SIZE = 32
        HIDDEN_SIZE = 512
        MLP_DIM = 4096
        NVFP4_LUT = jnp.array([0.0, 0.5, 1.0, 1.5, 2.0, 3.0, 4.0, 6.0, 0.0, -0.5, -1.0, -1.5, -2.0, -3.0, -4.0, -6.0], dtype=jnp.float32)

        def dequant_nvfp4(W_packed, scales, block=BLOCK_SIZE):
            N = W_packed.shape[0]
            low = W_packed & 15
            high = W_packed >> 4 & 15
            idx = jnp.stack([low, high], axis=-1).reshape(N, -1)
            vals = NVFP4_LUT[idx]
            K = vals.shape[1]
            vals = vals.reshape(N, K // block, block) * scales[:, :, None]
            return vals.reshape(N, K)
        key = jax.random.key(seed)
        ks = jax.random.split(key, 7)
        x = jax.random.normal(ks[0], (4, 32, HIDDEN_SIZE), dtype=jnp.float32)
        gate_W_packed = jax.random.randint(ks[1], (MLP_DIM, HIDDEN_SIZE // 2), 0, 64, dtype=jnp.int32)
        gate_scales = jax.random.uniform(ks[2], (MLP_DIM, HIDDEN_SIZE // BLOCK_SIZE), dtype=jnp.float32) * 0.1 + 0.001
        up_W_packed = jax.random.randint(ks[3], (MLP_DIM, HIDDEN_SIZE // 2), 0, 64, dtype=jnp.int32)
        up_scales = jax.random.uniform(ks[4], (MLP_DIM, HIDDEN_SIZE // BLOCK_SIZE), dtype=jnp.float32) * 0.1 + 0.001
        down_W_packed = jax.random.randint(ks[5], (HIDDEN_SIZE, MLP_DIM // 2), 0, 64, dtype=jnp.int32)
        down_scales = jax.random.uniform(ks[6], (HIDDEN_SIZE, MLP_DIM // BLOCK_SIZE), dtype=jnp.float32) * 0.1 + 0.001
        return {'x': x, 'gate_W_packed': gate_W_packed, 'gate_scales': gate_scales, 'up_W_packed': up_W_packed, 'up_scales': up_scales, 'down_W_packed': down_W_packed, 'down_scales': down_scales}
    _L0_ffn_in = _L0_ffn_setup()
    _d = {'L0_attn_hidden_states': _L0_attn_in['hidden_states'], 'L0_attn_w_qkv': _L0_attn_in['w_qkv'], 'L0_attn_w_o': _L0_attn_in['w_o'], 'L0_ffn_gate_W_packed': _L0_ffn_in['gate_W_packed'], 'L0_ffn_gate_scales': _L0_ffn_in['gate_scales'], 'L0_ffn_up_W_packed': _L0_ffn_in['up_W_packed'], 'L0_ffn_up_scales': _L0_ffn_in['up_scales'], 'L0_ffn_down_W_packed': _L0_ffn_in['down_W_packed'], 'L0_ffn_down_scales': _L0_ffn_in['down_scales']}
    _x0 = _d['L0_attn_hidden_states']
    _d['L0_attn_hidden_states'] = jax.random.normal(jax.random.fold_in(jax.random.key(seed), 1), (1, 2048, 512), dtype=_x0.dtype)
    del _x0
    return _d

def reference(L0_attn_hidden_states, L0_attn_w_qkv, L0_attn_w_o, L0_ffn_gate_W_packed, L0_ffn_gate_scales, L0_ffn_up_W_packed, L0_ffn_up_scales, L0_ffn_down_W_packed, L0_ffn_down_scales):

    def _L0_attn_ref(hidden_states, w_qkv, w_o):
        import jax, jax.numpy as jnp
        import numpy as np
        E2M1_GRID = jnp.array([0.0, 0.5, 1.0, 1.5, 2.0, 3.0, 4.0, 6.0], dtype=jnp.float32)
        E2M1_MIDS = (E2M1_GRID[1:] + E2M1_GRID[:-1]) / 2.0
        FP4_MAX = 6.0
        FP8_E4M3_MAX = 448.0

        def nvfp4_quant_dequant(w):
            O, I = w.shape
            w16 = w.reshape(O, I // 128, 8, 16)
            amax128 = jnp.max(jnp.abs(w16), axis=(-2, -1))
            outer = amax128 / (FP4_MAX * FP8_E4M3_MAX)
            outer = jnp.where(outer > 0, outer, 1.0)
            amax16 = jnp.max(jnp.abs(w16), axis=-1)
            inner = amax16 / FP4_MAX / outer[..., None]
            inner = inner.astype(jnp.float8_e4m3fn).astype(jnp.float32)
            scale = outer[..., None] * inner
            safe = jnp.where(scale > 0, scale, 1.0)[..., None]
            code = w16 / safe
            a = jnp.abs(code)
            idx = jnp.searchsorted(E2M1_MIDS, a)
            q = E2M1_GRID[idx] * jnp.sign(code)
            return (q * scale[..., None]).reshape(O, I)
        B, S, H = hidden_states.shape
        num_heads = 16
        head_dim = H // num_heads
        qkv = jnp.einsum('bsh,oh->bso', hidden_states, w_qkv)
        qkv = qkv.reshape(B, S, 3, num_heads, head_dim)
        qkv = jnp.transpose(qkv, (2, 0, 3, 1, 4))
        q, k, v = (qkv[0], qkv[1], qkv[2])
        scale = 1.0 / jnp.sqrt(jnp.float32(head_dim))
        scores = jnp.einsum('bhqd,bhkd->bhqk', q, k) * scale
        causal = jnp.tril(jnp.ones((S, S), dtype=bool))
        scores = jnp.where(causal, scores, jnp.finfo(scores.dtype).min)
        probs = jax.nn.softmax(scores, axis=-1)
        attn = jnp.einsum('bhqk,bhkd->bhqd', probs, v)
        attn = jnp.transpose(attn, (0, 2, 1, 3)).reshape(B, S, H)
        return jnp.einsum('bsh,oh->bso', attn, w_o)

    def _L0_ffn_ref(x, gate_W_packed, gate_scales, up_W_packed, up_scales, down_W_packed, down_scales):
        import jax, jax.numpy as jnp
        import numpy as np
        BLOCK_SIZE = 32
        HIDDEN_SIZE = 512
        MLP_DIM = 4096
        NVFP4_LUT = jnp.array([0.0, 0.5, 1.0, 1.5, 2.0, 3.0, 4.0, 6.0, 0.0, -0.5, -1.0, -1.5, -2.0, -3.0, -4.0, -6.0], dtype=jnp.float32)

        def dequant_nvfp4(W_packed, scales, block=BLOCK_SIZE):
            N = W_packed.shape[0]
            low = W_packed & 15
            high = W_packed >> 4 & 15
            idx = jnp.stack([low, high], axis=-1).reshape(N, -1)
            vals = NVFP4_LUT[idx]
            K = vals.shape[1]
            vals = vals.reshape(N, K // block, block) * scales[:, :, None]
            return vals.reshape(N, K)
        B, S, H = x.shape
        xt = x.reshape(B * S, H)
        Wg = dequant_nvfp4(gate_W_packed, gate_scales)
        Wu = dequant_nvfp4(up_W_packed, up_scales)
        Wd = dequant_nvfp4(down_W_packed, down_scales)
        gate = jnp.einsum('th,nh->tn', xt, Wg)
        up = jnp.einsum('th,nh->tn', xt, Wu)
        gelu = jnp.tanh(0.7978845608028654 * (gate + 0.044715 * gate ** 3)) * gate * 0.5 + gate * 0.5
        inter = gelu * up
        out = jnp.einsum('tn,hn->th', inter, Wd)
        return out.reshape(B, S, H)
    x = L0_attn_hidden_states
    xn = _layernorm(x, axis=-1)
    x = x + _L0_attn_ref(xn, L0_attn_w_qkv, L0_attn_w_o) + _L0_ffn_ref(xn, L0_ffn_gate_W_packed, L0_ffn_gate_scales, L0_ffn_up_W_packed, L0_ffn_up_scales, L0_ffn_down_W_packed, L0_ffn_down_scales)
    return x

_drawn_inputs = setup_inputs


def setup_inputs(seed=0):
    import zlib

    import numpy as np

    out = dict(_drawn_inputs(seed))
    spreads = {}
    factors = {'L0_attn_w_qkv': 8.0, 'L0_attn_w_o': 8.0}
    for name, (base, spread) in spreads.items():
        noise = np.random.default_rng([zlib.crc32(name.encode()), seed]).standard_normal(out[name].shape)
        drawn = base * np.exp(spread * noise) if base else spread * noise
        out[name] = jnp.asarray(drawn.astype(out[name].dtype))
    for name, factor in factors.items():
        out[name] = (out[name] * factor).astype(out[name].dtype)
    return out
```

```python
import numpy as np
import concourse.bass as bass
from concourse import mybir
from contextlib import ExitStack

F32 = mybir.dt.float32
F32R = mybir.dt.float32r
BF16 = mybir.dt.bfloat16
F16 = mybir.dt.float16
I32 = mybir.dt.int32
ALU = mybir.AluOpType
ACT = mybir.ActivationFunctionType
AX = mybir.AxisListType

P = 128
S = 2048
H = 512
NH = 16
D = H // NH
MLP = 4096
KT = H // P
TT = S // P
W = 512
TC = S // W
EPS = 1e-5
MASKED = -float(2 ** 100)
NO_MAX = -3.0e38
SCALE = 1.0 / float(np.sqrt(np.float32(D)))


def mm3(nc, out, w_hi, w_lo, x_hi, x_lo, first, last):
    nc.tensor.matmul(out, w_hi, x_hi, start=first, stop=False)
    nc.tensor.matmul(out, w_hi, x_lo, start=False, stop=False)
    return nc.tensor.matmul(out, w_lo, x_hi, start=False, stop=last)


def norm_and_project(nc, x, wqkv_t, qk_scratch, v_scratch, xn_hi, xn_lo):
    LOADS = 4
    PER = TT // LOADS
    UNITS_QK = 2 * KT * TC
    UNITS = UNITS_QK + TT
    SLOTS = 4
    with ExitStack() as ctx:
        def sb(name, shape, dt):
            return ctx.enter_context(nc.sbuf_tensor(name, shape, dt))

        def sem(name):
            return ctx.enter_context(nc.semaphore(name))

        x_sb = sb("x_sb", [P, TT, H], F32)
        w_sb = sb("wqkv_sb", [P, KT, 3 * H], F32)
        w_hi = sb("wqkv_hi", [P, KT, 3 * H], F32R)
        w_lo = sb("wqkv_lo", [P, KT, 3 * H], F32R)
        ident = sb("ident1", [P, P], F32)
        stats = sb("stats", [P, TT, 6], F32)
        mean_var = sb("mean_var", [P, TT, 2], F32)
        var_eps = sb("var_eps", [P, TT], F32)
        std = sb("std", [P, TT], F32)
        rstd = sb("rstd", [P, TT], F32)
        out_hi = sb("out_hi", [P, SLOTS, W], F32R)
        out_lo = sb("out_lo", [P, SLOTS, W], F32R)
        out_v = sb("out_v", [P, 2, NH, 2, D], F32R)
        pt = ctx.enter_context(nc.psum_tensor("pt", [P, 2, W], F32))
        pj = ctx.enter_context(nc.psum_tensor("pj", [P, SLOTS, W], F32))

        x_loaded = [sem(f"x_loaded{i}") for i in range(LOADS)]
        w_loaded = [sem(f"w_loaded{i}") for i in range(3)]
        ident_made = sem("ident_made")
        stats_made = sem("stats_made")
        std_made = sem("std_made")
        rstd_made = sem("rstd_made")
        xn_made = sem("xn_made")
        transposed = sem("transposed")
        xn_hi_made = sem("xn_hi_made")
        xn_lo_made = sem("xn_lo_made")
        w_hi_made = sem("w_hi_made")
        w_lo_made = sem("w_lo_made")
        projected = sem("projected")
        hi_made = sem("hi_made")
        lo_made = sem("lo_made")
        stored = [sem(f"stored{i}") for i in range(SLOTS)]
        stored_v = [sem(f"stored_v{i}") for i in range(2)]
        block = ctx.enter_context(nc.Block())

        @block.sync
        def _(sp):
            for i in range(LOADS):
                sp.dma_start(x_sb[:, i * PER:(i + 1) * PER, :],
                             x[i * PER * P:(i + 1) * PER * P, :].rearrange("(t p) h -> p t h", p=P)
                             ).then_inc(x_loaded[i], 16)
                if i < 3:
                    sp.dma_start(w_sb[:, :, i * H:(i + 1) * H],
                                 wqkv_t[:, i * H:(i + 1) * H].rearrange("(k p) o -> p k o", p=P)
                                 ).then_inc(w_loaded[i], 16)
            for u in range(UNITS):
                sp.wait_ge(hi_made, u + 1)
                sp.wait_ge(lo_made, u + 1)
                if u < UNITS_QK:
                    ot, tc = divmod(u, TC)
                    rows = slice((ot % KT) * P, (ot % KT + 1) * P)
                    for part, tile in ((0, out_hi), (1, out_lo)):
                        sp.dma_start(qk_scratch[ot // KT, part, rows, tc * W:(tc + 1) * W],
                                     tile[:, u % SLOTS, :].bitcast(F32)).then_inc(stored[u % SLOTS], 16)
                else:
                    tt = u - UNITS_QK
                    sp.dma_start(v_scratch[tt * P:(tt + 1) * P, :, :],
                                 out_v[:, tt % 2, :, :, :].rearrange("p h a d -> p h (a d)").bitcast(F32)
                                 ).then_inc(stored_v[tt % 2], 16)
            for s in range(SLOTS):
                sp.wait_ge(stored[s], 32 * (UNITS_QK // SLOTS))
            for s in range(2):
                sp.wait_ge(stored_v[s], 16 * (TT // 2))

        @block.gpsimd
        def _(pool):
            nc.gpsimd.memset(ident[:, :], 0.0).then_inc(ident_made, 1)
            pool.wait_ge(ident_made, 1)
            nc.gpsimd.affine_select(out=ident[:, :], in_=ident[:, :], compare_op=ALU.not_equal, fill=1.0,
                                    base=0, pattern=[[-1, P]], channel_multiplier=1).then_inc(ident_made, 1)

        @block.scalar
        def _(act):
            for i in range(LOADS):
                act.wait_ge(stats_made, (2 * PER + 1) * (i + 1))
                cols = slice(i * PER, (i + 1) * PER)
                nc.scalar.activation(std[:, cols], var_eps[:, cols], ACT.Sqrt).then_inc(std_made, 1)
            for i in range(3):
                act.wait_ge(w_loaded[i], 16)
                nc.scalar.activation(w_hi[:, :, i * H:(i + 1) * H], w_sb[:, :, i * H:(i + 1) * H],
                                     ACT.Copy).then_inc(w_hi_made, 1)
            for tt in range(TT):
                act.wait_ge(transposed, tt + 1)
                nc.scalar.activation(xn_hi[:, :, tt * P:(tt + 1) * P],
                                     pt[:, tt % 2, :].rearrange("p (k t) -> p k t", k=KT),
                                     ACT.Copy).then_inc(xn_hi_made, 1)
            for u in range(UNITS):
                act.wait_ge(projected, u + 1)
                if u < UNITS_QK:
                    if u >= SLOTS:
                        act.wait_ge(stored[u % SLOTS], 32 * (u // SLOTS))
                    nc.scalar.activation(out_hi[:, u % SLOTS, :], pj[:, u % SLOTS, :],
                                         ACT.Copy).then_inc(hi_made, 1)
                else:
                    tt = u - UNITS_QK
                    if tt >= 2:
                        act.wait_ge(stored_v[tt % 2], 16 * (tt // 2))
                    nc.scalar.activation(out_v[:, tt % 2, :, 0, :],
                                         pj[:, u % SLOTS, :].rearrange("p (h d) -> p h d", h=NH),
                                         ACT.Copy).then_inc(hi_made, 1)

        @block.vector
        def _(dve):
            n = 0
            for i in range(LOADS):
                dve.wait_ge(x_loaded[i], 16)
                for tt in range(i * PER, (i + 1) * PER):
                    nc.vector.bn_stats(stats[:, tt, :], x_sb[:, tt, :]).then_inc(stats_made, 1)
                n += PER
                for tt in range(i * PER, (i + 1) * PER):
                    dve.wait_ge(stats_made, n)
                    nc.vector.bn_aggr(mean_var[:, tt, :], stats[:, tt, :])\
                        .then_inc(stats_made, 1)
                    n += 1
                dve.wait_ge(stats_made, n)
                cols = slice(i * PER, (i + 1) * PER)
                nc.vector.tensor_scalar(var_eps[:, cols], mean_var[:, cols, 1], EPS, None,
                                        ALU.add).then_inc(stats_made, 1)
                n += 1
                dve.wait_ge(std_made, i + 1)
                nc.vector.reciprocal(rstd[:, cols], std[:, cols]).then_inc(rstd_made, 1)
                dve.wait_ge(rstd_made, i + 1)
                for tt in range(i * PER, (i + 1) * PER):
                    nc.vector.tensor_scalar(x_sb[:, tt, :], x_sb[:, tt, :], mean_var[:, tt, 0:1],
                                            rstd[:, tt:tt + 1], ALU.subtract, ALU.mult).then_inc(xn_made, 1)
            for tt in range(TT):
                dve.wait_ge(xn_hi_made, tt + 1)
                cols = slice(tt * P, (tt + 1) * P)
                nc.vector.tensor_tensor(xn_lo[:, :, cols], pt[:, tt % 2, :].rearrange("p (k t) -> p k t", k=KT),
                                        xn_hi[:, :, cols].bitcast(F32), ALU.subtract).then_inc(xn_lo_made, 1)
                if tt % 4 == 3 and tt // 4 < 3:
                    i = tt // 4
                    dve.wait_ge(w_hi_made, i + 1)
                    cols = slice(i * H, (i + 1) * H)
                    nc.vector.tensor_tensor(w_lo[:, :, cols], w_sb[:, :, cols], w_hi[:, :, cols].bitcast(F32),
                                            ALU.subtract).then_inc(w_lo_made, 1)
            for u in range(UNITS):
                dve.wait_ge(hi_made, u + 1)
                if u < UNITS_QK:
                    nc.vector.tensor_tensor(out_lo[:, u % SLOTS, :], pj[:, u % SLOTS, :],
                                            out_hi[:, u % SLOTS, :].bitcast(F32), ALU.subtract).then_inc(lo_made, 1)
                else:
                    tt = u - UNITS_QK
                    nc.vector.tensor_tensor(out_v[:, tt % 2, :, 1, :],
                                            pj[:, u % SLOTS, :].rearrange("p (h d) -> p h d", h=NH),
                                            out_v[:, tt % 2, :, 0, :].bitcast(F32), ALU.subtract).then_inc(lo_made, 1)

        @block.tensor
        def _(pe):
            pe.wait_ge(ident_made, 2)
            for tt in range(TT):
                pe.wait_ge(xn_made, tt + 1)
                if tt >= 2:
                    pe.wait_ge(xn_lo_made, tt - 1)
                for kt in range(KT):
                    par, half = divmod(kt, 2)
                    first = 2 * P * half + par
                    last = nc.tensor.transpose(pt[:, tt % 2, kt * P:(kt + 1) * P],
                                               x_sb[:, tt, first:first + 2 * P - 1:2], ident[:, :])
                last.then_inc(transposed, 1)
            pe.wait_ge(xn_lo_made, TT)
            for u in range(UNITS):
                if u % (KT * TC) == 0:
                    pe.wait_ge(w_lo_made, u // (KT * TC) + 1)
                if u >= SLOTS:
                    pe.wait_ge(lo_made, u - SLOTS + 1)
                for kt in range(KT):
                    if u < UNITS_QK:
                        ot, tc = divmod(u, TC)
                        o, t = slice(ot * P, (ot + 1) * P), slice(tc * W, (tc + 1) * W)
                        last = mm3(nc, pj[:, u % SLOTS, :], w_hi[:, kt, o], w_lo[:, kt, o],
                                   xn_hi[:, kt, t], xn_lo[:, kt, t], kt == 0, kt == KT - 1)
                    else:
                        tt = u - UNITS_QK
                        o, t = slice(2 * H, 3 * H), slice(tt * P, (tt + 1) * P)
                        last = mm3(nc, pj[:, u % SLOTS, :], xn_hi[:, kt, t], xn_lo[:, kt, t],
                                   w_hi[:, kt, o], w_lo[:, kt, o], kt == 0, kt == KT - 1)
                last.then_inc(projected, 1)


def attention(nc, qk_scratch, v_scratch, sum_scratch, attn_t):
    GROUP = 4
    ROWS = 3 * D
    VW = 3 * D
    CAP = 2 * W
    UNITS = [(i, k, min(CAP, P * (i + 1) - k)) for i in range(TT) for k in range(0, P * (i + 1), CAP)]
    NU = len(UNITS)
    STEPS = [(qc, pair, 0 if pair < 2 * qc + 1 else W // 2) for qc in range(TC) for pair in range(2 * qc + 2)]
    NS = len(STEPS)
    LAST = [s for s in range(NS) if s + 1 == NS or STEPS[s + 1][0] != STEPS[s][0]]
    BESIDE = {s: [] for s in range(NS)}
    for u in range(NU):
        BESIDE[4 + u * (NS - 8) // NU].append(u)
    CHAIN = NS - 4
    ON_POOL = [s % 4 == 3 for s in range(NS)]
    PER_POOL = sum(ON_POOL)
    PER_DVE = NS - PER_POOL
    CREDIT = 4

    def lo_count(s, pool):
        whole, part = divmod(s, NS)
        return whole * (PER_POOL if pool else PER_DVE) + sum(p == pool for p in ON_POOL[:part + 1])

    with ExitStack() as ctx:
        def sb(name, shape, dt):
            return ctx.enter_context(nc.sbuf_tensor(name, shape, dt))

        def sem(name):
            return ctx.enter_context(nc.semaphore(name))

        q_stack = [sb(f"q_stack{i}", [P, S], F32R) for i in range(2)]
        k_stack = [sb(f"k_stack{i}", [P, S], F32R) for i in range(2)]
        v_stack = [sb(f"v_stack{i}", [P, TT, VW], F32R) for i in range(2)]
        e_sb = sb("e_sb", [P, 2, 2, W], F32)
        e_hi = sb("e_hi", [P, 2, 2, W], F32R)
        e_lo = sb("e_lo", [P, 2, 2, W], F32R)
        lo_sum = sb("lo_sum", [D + 1, 2, TC, W], F32)
        max_part = sb("max_part", [P, TT, 2], F32)
        row_max = sb("row_max", [P, TT], F32)
        rest1 = sb("rest1", [P, TT], F32)
        rest2 = sb("rest2", [P, TT], F32)
        max_cols = sb("max_cols", [P, TT, P], BF16)
        ident = sb("ident_bf", [P, P], BF16)
        mask_q = sb("mask_q", [P, P], BF16)
        mask_k = sb("mask_k", [P, 2 * P], BF16)
        p_st = ctx.enter_context(nc.psum_tensor("p_st", [P, 2, 2, W], F32))
        p_s = ctx.enter_context(nc.psum_tensor("p_s", [P, 2, W], F32))
        p_o = ctx.enter_context(nc.psum_tensor("p_o", [P, W], F32))
        p_m = ctx.enter_context(nc.psum_tensor("p_m", [P, W], F32))

        consts = sem("consts")
        minus_one = sem("minus_one")
        pool_turns = sem("pool_turns_attn")
        qk_loaded = [sem(f"qk_loaded{i}") for i in range(2)]
        v_loaded = [sem(f"v_loaded{i}") for i in range(2)]
        scored = sem("scored")
        maxed = sem("maxed")
        max_step = sem("max_step")
        max_split = sem("max_split")
        max_turned = sem("max_turned")
        max_rows = sem("max_rows")
        st_ready = sem("st_ready")
        exp_done = sem("exp_done")
        hi_made = sem("e_hi_made")
        lo_made = {False: sem("e_lo_made_dve"), True: sem("e_lo_made_pool")}
        pv_done = sem("pv_done")
        lo_sum_made = sem("lo_sum_made")
        o_free = sem("o_free")
        sums_out = [sem(f"sums_out{i}") for i in range(2)]
        block = ctx.enter_context(nc.Block())
        NC = 6

        def load_head(sp, h, par):
            rows = bass.ds(h * D, D)
            for strip, part in enumerate((0, 0, 1)):
                sp.dma_start(q_stack[par][strip * D:(strip + 1) * D, :].bitcast(F32),
                             qk_scratch[0, part, rows, :]).then_inc(qk_loaded[par], 16)
            for strip, part in enumerate((0, 1, 0)):
                sp.dma_start(k_stack[par][strip * D:(strip + 1) * D, :].bitcast(F32),
                             qk_scratch[1, part, rows, :]).then_inc(qk_loaded[par], 16)
            for part, col in ((0, 2 * D), (1, 0)):
                sp.dma_start(v_stack[par][:, :, col:col + D].bitcast(F32),
                             v_scratch[:, bass.ds(2 * h + part, 1), :].rearrange("(t p) a d -> p t (a d)", p=P)
                             ).then_inc(v_loaded[par], 16)

        @block.sync
        def _(sp):
            load_head(sp, 0, 0)
            load_head(sp, 1, 1)

            def group(g, last):
                for j in range(GROUP):
                    h = g * GROUP + j
                    if not (last and j >= GROUP - 2):
                        sp.wait_ge(pv_done, (h + 1) * NS + 2)
                        load_head(sp, h + 2, j % 2)
                    sp.wait_ge(lo_sum_made, (h + 1) * TC)
                    sp.dma_start(sum_scratch[bass.ds(h, 1), :],
                                 lo_sum[D:D + 1, j % 2, :, :].rearrange("p c w -> p (c w)")
                                 ).then_inc(sums_out[j % 2], 16)

            sp.sem_inc(sums_out[0], 16)
            sp.sem_inc(sums_out[1], 16)
            with sp.Fori(0, NH // GROUP - 1) as g:
                group(g, False)
            group(NH // GROUP - 1, True)
            for s in sums_out:
                sp.wait_ge(s, 16 * (NH // 2 + 1))

        @block.gpsimd
        def _(pool):
            nc.gpsimd.memset(ident[:, :], 0.0).then_inc(consts, 1)
            nc.gpsimd.memset(mask_q[:, :], 0.0).then_inc(consts, 1)
            nc.gpsimd.memset(mask_k[:, 0:P], MASKED).then_inc(consts, 1)
            nc.gpsimd.memset(mask_k[:, P:], 0.0).then_inc(consts, 1)
            nc.gpsimd.memset(max_cols[:, :, :], 0.0).then_inc(consts, 1)
            nc.gpsimd.memset(max_part[:, :, :], NO_MAX).then_inc(consts, 1)
            pool.wait_ge(consts, NC)
            nc.gpsimd.affine_select(out=ident[:, :], in_=ident[:, :], compare_op=ALU.not_equal, fill=1.0,
                                    base=0, pattern=[[-1, P]], channel_multiplier=1).then_inc(consts, 1)
            nc.gpsimd.affine_select(out=mask_q[:, :], in_=mask_q[:, :], compare_op=ALU.is_ge, fill=MASKED,
                                    base=0, pattern=[[-1, P]], channel_multiplier=1).then_inc(consts, 1)
            nc.gpsimd.affine_select(out=mask_k[:, P:], in_=mask_k[:, P:], compare_op=ALU.is_ge, fill=MASKED,
                                    base=0, pattern=[[1, P]], channel_multiplier=-1).then_inc(consts, 1)
            pool.wait_ge(consts, NC + 3)
            pool.sem_inc(hi_made, 2)
            pool.sem_inc(lo_made[True], CREDIT)

            def group(g):
                for j in range(GROUP):
                    h = g * GROUP + j
                    for s, (qc, pair, q0) in enumerate(STEPS):
                        n = h * NS + s
                        w = W - q0
                        pool.wait_ge(exp_done, n + 3)
                        pool.wait_ge(pv_done, n + 1)
                        pool.sem_inc(pool_turns, 1)
                        nc.gpsimd.tensor_copy(e_hi[:, s % 2, :, 0:w], e_sb[:, s % 2, :, 0:w]).then_inc(hi_made, 1)
                        if ON_POOL[s]:
                            pool.wait_ge(hi_made, n + 3)
                            nc.gpsimd.tensor_tensor(e_lo[:, s % 2, :, 0:w], e_sb[:, s % 2, :, 0:w],
                                                    e_hi[:, s % 2, :, 0:w].bitcast(F32),
                                                    ALU.subtract).then_inc(lo_made[True], 1)

            with pool.Fori(0, NH // GROUP - 1) as g:
                group(g)
            group(NH // GROUP - 1)

        @block.scalar
        def _(act):
            def max_row(h, par, r):
                act.wait_ge(max_turned, h * TC + r + 1)
                nc.scalar.activation(q_stack[par][ROWS:P, r * W:(r + 1) * W], p_m[ROWS:P, :],
                                     ACT.Copy).then_inc(max_rows, 1)

            def exps(h, s):
                qc, pair, q0 = STEPS[s]
                w = W - q0
                act.wait_ge(st_ready, h * NS + s + 1)
                act.wait_ge(hi_made, h * NS + s + 1)
                for on_pool, per in ((False, PER_DVE), (True, PER_POOL)):
                    act.wait_ge(lo_made[on_pool], h * per + lo_count(s - 2, on_pool) + CREDIT)
                nc.scalar.activation(e_sb[:, s % 2, :, 0:w], p_st[:, s % 2, :, 0:w], ACT.Exp,
                                     scale=SCALE).then_inc(exp_done, 1)

            act.sem_inc(exp_done, 2)
            for r in range(TC):
                max_row(0, 0, r)
            exps(0, 0)

            def group(g, last):
                for j in range(GROUP):
                    h = g * GROUP + j
                    final = last and j == GROUP - 1
                    for s in range(NS):
                        if s + 1 < NS:
                            exps(h, s + 1)
                        elif not final:
                            exps(h + 1, 0)
                        if s >= NS - 3 and not final:
                            max_row(h + 1, (j + 1) % 2, s - (NS - 3))
                        if s in LAST:
                            qc = STEPS[s][0]
                            act.wait_ge(pv_done, h * NS + s + 3)
                            if qc == 0:
                                act.wait_ge(sums_out[j % 2], (g * 2 + j // 2 + 1) * 16)
                            nc.scalar.activation(lo_sum[:, j % 2, qc, :], p_o[0:D + 1, :],
                                                 ACT.Copy).then_inc(lo_sum_made, 1)
                    if not final:
                        max_row(h + 1, (j + 1) % 2, TC - 1)

            with act.Fori(0, NH // GROUP - 1) as g:
                group(g, False)
            group(NH // GROUP - 1, True)

        @block.vector
        def _(dve):
            for par in range(2):
                nc.vector.memset(k_stack[par][ROWS:P, :].bitcast(F32), 0.0).then_inc(minus_one, 1)
                nc.vector.memset(v_stack[par][:, :, D:2 * D].bitcast(F32), 0.0).then_inc(minus_one, 1)
            dve.wait_ge(minus_one, 4)
            for par in range(2):
                nc.vector.memset(k_stack[par][ROWS:ROWS + 3, :].bitcast(F32), -1.0).then_inc(minus_one, 1)
                nc.vector.memset(v_stack[par][:, :, D:D + 1].bitcast(F32), 1.0).then_inc(minus_one, 1)
            dve.wait_ge(consts, NC)
            dve.sem_inc(lo_made[False], CREDIT)
            dve.sem_inc(o_free, 1)

            def unit_max(h, u):
                i, k, w = UNITS[u]
                dve.wait_ge(scored, h * NU + u + 1)
                nc.vector.reduce_max(max_part[:, i, k // CAP:k // CAP + 1],
                                     p_s[:, :, :].rearrange("p b w -> p (b w)")[:, 0:w],
                                     AX.X).then_inc(maxed, 1)

            def split_max(h, first=False):
                dve.wait_ge(maxed, (h + 1) * NU + 1)
                if not first:
                    dve.wait_ge(max_turned, h * TC)
                nc.vector.reduce_max(row_max[:, :], max_part[:, :, :], AX.X).then_inc(max_step, 1)
                dve.wait_ge(max_step, h * 5 + 1)
                nc.vector.tensor_copy(max_cols[:, :, ROWS], row_max[:, :]).then_inc(max_step, 1)
                dve.wait_ge(max_step, h * 5 + 2)
                nc.vector.tensor_tensor(rest1[:, :], row_max[:, :], max_cols[:, :, ROWS],
                                        ALU.subtract).then_inc(max_step, 1)
                dve.wait_ge(max_step, h * 5 + 3)
                nc.vector.tensor_copy(max_cols[:, :, ROWS + 1], rest1[:, :]).then_inc(max_step, 1)
                dve.wait_ge(max_step, h * 5 + 4)
                nc.vector.tensor_tensor(rest2[:, :], rest1[:, :], max_cols[:, :, ROWS + 1],
                                        ALU.subtract).then_inc(max_step, 1)
                dve.wait_ge(max_step, h * 5 + 5)
                nc.vector.tensor_copy(max_cols[:, :, ROWS + 2], rest2[:, :]).then_inc(max_split, 1)

            def add_parts(g, h, j, qc):
                dve.wait_ge(lo_sum_made, h * TC + qc + 1)
                nc.vector.tensor_tensor(attn_t[j * D:(j + 1) * D, bass.ds(g * S + qc * W, W)],
                                        p_o[2 * D:VW, :], lo_sum[0:D, j % 2, qc, :],
                                        ALU.add).then_inc(o_free, 1)

            for u in range(NU):
                unit_max(0, u)
            split_max(0, first=True)

            def group(g, last):
                for j in range(GROUP):
                    h = g * GROUP + j
                    final = last and j == GROUP - 1
                    for s, (qc, pair, q0) in enumerate(STEPS):
                        n = h * NS + s
                        w = W - q0
                        if not final:
                            for u in BESIDE[s]:
                                unit_max(h + 1, u)
                        if s - 1 in LAST:
                            add_parts(g, h, j, STEPS[s - 1][0])
                        if s == CHAIN and not final:
                            split_max(h + 1)
                        if not ON_POOL[s]:
                            dve.wait_ge(hi_made, n + 3)
                            dve.wait_ge(pv_done, n + 1)
                            nc.vector.tensor_tensor(e_lo[:, s % 2, :, 0:w], e_sb[:, s % 2, :, 0:w],
                                                    e_hi[:, s % 2, :, 0:w].bitcast(F32),
                                                    ALU.subtract).then_inc(lo_made[False], 1)
                    add_parts(g, h, j, TC - 1)

            with dve.Fori(0, NH // GROUP - 1) as g:
                group(g, False)
            group(NH // GROUP - 1, True)

        @block.tensor
        def _(pe):
            pe.sem_inc(pv_done, 2)
            pe.wait_ge(consts, NC + 3)
            pe.wait_ge(minus_one, 8)

            def scores(h, par, u):
                i, k, w = UNITS[u]
                pe.wait_ge(maxed, h * NU + u + 1)
                for b in range(0, w, W):
                    wb = min(W, w - b)
                    diagonal = k + b + wb == P * (i + 1)
                    last = nc.tensor.matmul(p_s[:, b // W, 0:wb], q_stack[par][0:ROWS, i * P:(i + 1) * P],
                                            k_stack[par][0:ROWS, k + b:k + b + wb], start=True, stop=not diagonal)
                    if diagonal:
                        last = nc.tensor.matmul(p_s[:, b // W, wb - P:wb], ident[:, :], mask_q[:, :],
                                                start=False, stop=True)
                last.then_inc(scored, 1)

            def turn_max(h, r):
                if r == 0:
                    pe.wait_ge(max_split, h + 1)
                pe.wait_ge(max_rows, h * TC + r + 1)
                for t in range(W // P):
                    last = nc.tensor.matmul(p_m[:, t * P:(t + 1) * P], max_cols[:, r * (W // P) + t, :],
                                            ident[:, :], start=True, stop=True)
                last.then_inc(max_turned, 1)

            def scores_t(h, par, s):
                qc, pair, q0 = STEPS[s]
                w = W - q0
                if pair == 0:
                    pe.wait_ge(max_rows, h * TC + qc + 2)
                pe.wait_ge(exp_done, h * NS + s + 1)
                for t in range(2):
                    kt = 2 * pair + t
                    diagonal = kt * P >= qc * W
                    last = nc.tensor.matmul(p_st[:, s % 2, t, 0:w], k_stack[par][:, kt * P:(kt + 1) * P],
                                            q_stack[par][:, qc * W + q0:(qc + 1) * W], start=True,
                                            stop=not diagonal)
                    if diagonal:
                        last = nc.tensor.matmul(p_st[:, s % 2, t, 0:(t + 1) * P], ident[:, :],
                                                mask_k[:, (1 - t) * P:], start=False, stop=True)
                last.then_inc(st_ready, 1)

            def product_v(h, par, s):
                qc, pair, q0 = STEPS[s]
                w = W - q0
                n = h * NS + s
                if pair == 0:
                    pe.wait_ge(o_free, h * TC + qc + 1)
                pe.wait_ge(hi_made, n + 3)
                pool = ON_POOL[s]
                final_step = s in LAST
                for part, tile in ((0, e_hi), (1, e_lo)):
                    if part:
                        pe.wait_ge(lo_made[pool], h * (PER_POOL if pool else PER_DVE) + lo_count(s, pool) + CREDIT)
                    for t in range(2):
                        last = nc.tensor.matmul(p_o[0:VW, q0:], v_stack[par][:, 2 * pair + t, :],
                                                tile[:, s % 2, t, 0:w], start=(pair == 0 and part == 0 and t == 0),
                                                stop=(final_step and part == 1 and t == 1))
                last.then_inc(pv_done, 1)

            def wait_qk(h_half, par):
                pe.wait_ge(qk_loaded[par], (h_half + 1) * 96)

            pe.sem_inc(maxed, 1)
            pe.sem_inc(max_rows, 1)
            wait_qk(0, 0)
            for u in range(NU):
                scores(0, 0, u)
            for r in range(TC):
                turn_max(0, r)
            scores_t(0, 0, 0)

            def group(g, last):
                for j in range(GROUP):
                    h = g * GROUP + j
                    par, other = j % 2, (j + 1) % 2
                    final = last and j == GROUP - 1
                    pe.wait_ge(v_loaded[par], (g * 2 + j // 2 + 1) * 32)
                    for s in range(NS):
                        if BESIDE[s] and BESIDE[s][0] == 0 and not final:
                            wait_qk(g * 2 + (j + 1) // 2, other)
                        if s + 1 < NS:
                            scores_t(h, par, s + 1)
                        elif not final:
                            scores_t(h + 1, other, 0)
                        if not final:
                            for u in BESIDE[s]:
                                scores(h + 1, other, u)
                            if s >= NS - 3:
                                turn_max(h + 1, s - (NS - 3))
                        product_v(h, par, s)
                    if not final:
                        turn_max(h + 1, TC - 1)

            with pe.Fori(0, NH // GROUP - 1) as g:
                group(g, False)
            group(NH // GROUP - 1, True)


def output_projection(nc, x_t, wo_t, sum_scratch, rsum_scratch, acc):
    SUMS = NH * S // P
    with ExitStack() as ctx:
        def sb(name, shape, dt):
            return ctx.enter_context(nc.sbuf_tensor(name, shape, dt))

        def sem(name):
            return ctx.enter_context(nc.semaphore(name))

        sums = sb("sums", [P, SUMS], F32)
        rsums = sb("rsums", [P, SUMS], F32)
        wo_sb = sb("wo_sb", [P, KT, H], F32)
        rows = sb("rsum_rows", [P, NH // 4, S], F32)
        xt_sb = sb("xt_sb", [P, KT, S], F32)
        po = ctx.enter_context(nc.psum_tensor("po", [P, 2, KT, W], F32))
        loaded = sem("sums_loaded")
        wo_loaded = sem("wo_loaded")
        x_loaded = sem("xt_loaded")
        inverted = sem("inverted")
        stored = sem("rsums_stored")
        rows_loaded = [sem(f"rows_loaded{g}") for g in range(NH // 4)]
        normalised = sem("normalised")
        projected = sem("o_projected")
        added = sem("o_added")
        block = ctx.enter_context(nc.Block())

        @block.sync
        def _(sp):
            sp.dma_start(sums[:, :], sum_scratch.rearrange("h (a b) -> (h a) b", b=SUMS)).then_inc(loaded, 16)
            sp.dma_start(wo_sb[:, :, :], wo_t.rearrange("(k p) o -> p k o", p=P)).then_inc(wo_loaded, 16)
            sp.dma_start(xt_sb[:, :, :], x_t.rearrange("(k p) t -> p k t", p=P)).then_inc(x_loaded, 16)
            sp.wait_ge(inverted, 1)
            sp.dma_start(rsum_scratch.rearrange("h (a b) -> (h a) b", b=SUMS), rsums[:, :]).then_inc(stored, 16)
            sp.wait_ge(stored, 16)
            for g in range(NH // 4):
                for j in range(4):
                    sp.dma_start(rows[j * D:(j + 1) * D, g, :],
                                 rsum_scratch[4 * g + j, :].partition_broadcast(D)).then_inc(rows_loaded[g], 16)

        @block.vector
        def _(dve):
            dve.wait_ge(loaded, 16)
            nc.vector.reciprocal(rsums[:, :], sums[:, :]).then_inc(inverted, 1)
            for g in range(NH // 4):
                dve.wait_ge(rows_loaded[g], 64)
                cols = slice(g * S, (g + 1) * S)
                nc.vector.tensor_tensor(acc[:, cols], acc[:, cols], rows[:, g, :],
                                        ALU.mult).then_inc(normalised, 1)
            dve.wait_ge(x_loaded, 16)
            for tc in range(TC):
                dve.wait_ge(projected, tc + 1)
                t = slice(tc * W, (tc + 1) * W)
                nc.vector.tensor_tensor(acc[:, :].rearrange("p (k t) -> p k t", k=KT)[:, :, t], xt_sb[:, :, t],
                                        po[:, tc % 2, :, :], ALU.add).then_inc(added, 1)

        @block.tensor
        def _(pe):
            pe.wait_ge(wo_loaded, 16)
            pe.wait_ge(normalised, NH // 4)
            for tc in range(TC):
                if tc >= 2:
                    pe.wait_ge(added, tc - 1)
                for ot in range(KT):
                    for g in range(NH // 4):
                        last = nc.tensor.matmul(po[:, tc % 2, ot, :], wo_sb[:, g, ot * P:(ot + 1) * P],
                                                acc[:, g * S + tc * W:g * S + (tc + 1) * W],
                                                start=g == 0, stop=g == NH // 4 - 1)
                last.then_inc(projected, 1)


def feed_forward(nc, gate_p, up_p, gate_up_s, down_p, down_s, xn_hi, xn_lo, acc, out_t):
    CN = 2 * P
    CHUNKS = MLP // CN
    PAIR = 2
    ROUND = PAIR * TC
    NB = 8
    REP = P // NB
    GELU_A = 0.044715
    GELU_B = 0.7978845608028654
    CODE_SCALE = float(2 ** 14)
    with ExitStack() as ctx:
        acc = acc[:, :].rearrange("p (k t) -> p k t", k=KT)

        def sb(name, shape, dt):
            return ctx.enter_context(nc.sbuf_tensor(name, shape, dt))

        def sem(name):
            return ctx.enter_context(nc.semaphore(name))

        packed = [sb(f"packed{i}", [P, 3, W], I32) for i in range(2)]
        scales = [sb(f"scales{i}", [P, 3, W], F32) for i in range(2)]
        high = sb("high", [P, W], I32)
        pair = sb("pair", [P, W], I32)
        magnitude = sb("magnitude", [P, W], I32)
        weight = sb("weight", [P, 2, W], F32)
        w_hi = [sb(f"w_hi{i}", [P, 3, 2, W], F32R) for i in range(2)]
        w_lo = [sb(f"w_lo{i}", [P, 3, 2, W], F32R) for i in range(2)]
        gate = sb("gate", [P, 2, W], F32)
        poly = sb("poly", [P, 2, W], F32)
        inter = sb("inter", [P, 2, W], F32)
        i_hi = sb("i_hi", [P, 2, 2, W], F32R)
        i_lo = sb("i_lo", [P, 2, 2, W], F32R)
        p_gate = ctx.enter_context(nc.psum_tensor("p_gate", [P, 2, W], F32))
        p_up = ctx.enter_context(nc.psum_tensor("p_up", [P, 2, W], F32))
        p_out = ctx.enter_context(nc.psum_tensor("p_out", [P, KT, W], F32))

        loaded = [sem(f"ffn_loaded{i}") for i in range(2)]
        unpacked = sem("unpacked")
        weight_hi = sem("weight_hi")
        weight_lo = sem("weight_lo")
        gate_done = sem("gate_done")
        up_done = sem("up_done")
        down_done = sem("down_done")
        gate_out = sem("gate_out")
        poly_done = sem("poly_done")
        pool_turns = sem("pool_turns")
        tanh_done = sem("tanh_done")
        gelu_done = sem("gelu_done")
        inter_done = sem("inter_done")
        i_hi_done = sem("i_hi_done")
        i_lo_done = sem("i_lo_done")
        added = sem("added")
        out_stored = sem("out_stored")
        block = ctx.enter_context(nc.Block())

        def load_chunk(sp, c, par):
            cols = bass.ds(c * CN, CN)
            for m, pk in enumerate((gate_p, up_p)):
                sp.dma_start(packed[par][:, m, :].rearrange("p (k n) -> p k n", k=2),
                             pk[:, cols].rearrange("(k p) n -> p k n", p=P)).then_inc(loaded[par], 16)
            sp.dma_start(packed[par][:, 2, :], down_p[bass.ds(c * P, P), :]).then_inc(loaded[par], 16)
            for b in range(NB):
                rows = slice(b * REP, (b + 1) * REP)
                sp.dma_start(scales[par][rows, 0:2, :].rearrange("p m (k n) -> p m k n", k=2),
                             gate_up_s[:, :, b, cols].partition_broadcast(REP)).then_inc(loaded[par], 16)
                sp.dma_start(scales[par][rows, 2, :], down_s[bass.ds(c * NB + b, 1), :].rearrange("a h -> (a h)")
                             .partition_broadcast(REP)).then_inc(loaded[par], 16)
        LOADED = 16 * (3 + 2 * NB)

        @block.sync
        def _(sp):
            load_chunk(sp, 0, 0)
            load_chunk(sp, 1, 1)

            def round_(i, last):
                for half in range(PAIR):
                    c = PAIR * i + half
                    if not last:
                        sp.wait_ge(weight_lo, 3 * (c + 1))
                        load_chunk(sp, c + 2, half)

            with sp.Fori(0, CHUNKS // PAIR - 1) as i:
                round_(i, False)
            for tc in range(TC):
                sp.wait_ge(added, (CHUNKS - 1) * TC + tc + 2)
                sp.dma_start(out_t[:, tc * W:(tc + 1) * W].rearrange("(k p) t -> p k t", p=P),
                             acc[:, :, tc * W:(tc + 1) * W]).then_inc(out_stored, 16)
            sp.wait_ge(out_stored, 16 * TC)

        def steps(eng, body):
            with eng.Fori(0, CHUNKS // PAIR - 1) as i:
                for j in range(ROUND):
                    body(i, j, False, j % TC == 3)
            for j in range(ROUND):
                body(CHUNKS // PAIR - 1, j, j == ROUND - 1, j % TC == 3 or j >= TC)

        def next_chunk(i, j):
            return PAIR * i + j // TC + 1, (j // TC + 1) % 2, i + 1 + j // TC

        @block.scalar
        def _(act):
            def hi_weights(c, par, m, first=False):
                act.wait_ge(unpacked, 7 * (3 * c + m + 1))
                if not first:
                    act.wait_ge(*((up_done, (c - 1) * TC + 1) if m < 2 else (down_done, (c - 1) * TC + 2)))
                nc.scalar.activation(w_hi[par][:, m, :, :], weight[:, :, :], ACT.Copy,
                                     scale=CODE_SCALE).then_inc(weight_hi, 1)

            def elementwise(n, buf):
                act.wait_ge(gate_done, n + 1)
                act.wait_ge(gelu_done, n + 1)
                nc.scalar.activation(gate[:, :, :], p_gate[:, :, :], ACT.Copy).then_inc(gate_out, 1)
                nc.scalar.activation(poly[:, :, :], p_gate[:, :, :], ACT.Square).then_inc(gate_out, 1)
                act.wait_ge(poly_done, 2 * n + 2)
                act.wait_ge(i_lo_done, n + 1)
                nc.scalar.activation(inter[:, :, :], poly[:, :, :], ACT.Tanh, scale=GELU_B).then_inc(tanh_done, 1)
                act.wait_ge(inter_done, n + 2)
                act.wait_ge(down_done, n + 1)
                nc.scalar.activation(i_hi[:, buf, :, :], inter[:, :, :], ACT.Copy).then_inc(i_hi_done, 1)

            def body(i, j, final, no_weights):
                if not no_weights:
                    c, par, _ = next_chunk(i, j)
                    hi_weights(c, par, j % TC)
                if not final:
                    elementwise(ROUND * i + j + 1, (j + 1) % 2)

            act.sem_inc(gate_out, 2)
            for m in range(3):
                hi_weights(0, 0, m, first=True)
            elementwise(0, 0)
            steps(act, body)

        @block.gpsimd
        def _(pool):
            def elementwise(n):
                pool.wait_ge(gate_out, 2 * n + 4)
                pool.sem_inc(pool_turns, 1)
                nc.gpsimd.tensor_scalar(poly[:, :, :], poly[:, :, :], GELU_A, 1.0, ALU.mult,
                                        ALU.add).then_inc(poly_done, 1)
                pool.wait_ge(poly_done, 2 * n + 1)
                nc.gpsimd.tensor_tensor(poly[:, :, :], poly[:, :, :], gate[:, :, :], ALU.mult).then_inc(poly_done, 1)

            def body(i, j, final, no_weights):
                if not final:
                    elementwise(ROUND * i + j + 1)

            elementwise(0)
            steps(pool, body)

        @block.vector
        def _(dve):
            def unpack(c, par, m, loads, first=False):
                k = 3 * c + m
                pk = packed[par][:, m, :]

                def own(step):
                    dve.wait_ge(unpacked, 7 * k + step)
                dve.wait_ge(loaded[par], LOADED * loads)
                if not (first and m == 0):
                    own(0)
                    dve.wait_ge(weight_lo, k)
                nc.vector.tensor_scalar(high[:, :], pk, 0xF0, 12, ALU.bitwise_and,
                                        ALU.logical_shift_left).then_inc(unpacked, 1)
                nc.vector.tensor_scalar(pair[:, :], pk, 0x0F, None, ALU.bitwise_and).then_inc(unpacked, 1)
                own(2)
                nc.vector.tensor_tensor(pair[:, :], pair[:, :], high[:, :], ALU.bitwise_or).then_inc(unpacked, 1)
                own(3)
                nc.vector.tensor_scalar(magnitude[:, :], pair[:, :], 0x00070007, 9, ALU.bitwise_and,
                                        ALU.logical_shift_left).then_inc(unpacked, 1)
                nc.vector.tensor_scalar(high[:, :], pair[:, :], 0x00080008, 12, ALU.bitwise_and,
                                        ALU.logical_shift_left).then_inc(unpacked, 1)
                own(5)
                nc.vector.tensor_tensor(magnitude[:, :], magnitude[:, :], high[:, :],
                                        ALU.bitwise_or).then_inc(unpacked, 1)
                own(6)
                codes = magnitude[:, :].bitcast(F16).rearrange("p (n a) -> p a n", a=2)
                sc = scales[par][:, m, :].unsqueeze(1).broadcast_to([P, 2, W])
                nc.vector.tensor_tensor(weight[:, :, :], codes, sc, ALU.mult).then_inc(unpacked, 1)

            def lo_weights(c, par, m):
                dve.wait_ge(weight_hi, 3 * c + m + 1)
                nc.vector.scalar_tensor_tensor(w_lo[par][:, m, :, :], weight[:, :, :], CODE_SCALE,
                                               w_hi[par][:, m, :, :].bitcast(F32), ALU.mult,
                                               ALU.subtract).then_inc(weight_lo, 1)

            def elementwise(n, buf):
                dve.wait_ge(tanh_done, n + 1)
                nc.vector.scalar_tensor_tensor(inter[:, :, :], inter[:, :, :], 1.0, gate[:, :, :],
                                               ALU.add, ALU.mult).then_inc(gelu_done, 1)
                dve.wait_ge(gelu_done, n + 2)
                dve.wait_ge(up_done, n + 2)
                nc.vector.scalar_tensor_tensor(inter[:, :, :], inter[:, :, :], 0.5, p_up[:, :, :],
                                               ALU.mult, ALU.mult).then_inc(inter_done, 1)
                dve.wait_ge(i_hi_done, n + 1)
                nc.vector.tensor_tensor(i_lo[:, buf, :, :], inter[:, :, :], i_hi[:, buf, :, :].bitcast(F32),
                                        ALU.subtract).then_inc(i_lo_done, 1)

            def body(i, j, final, no_weights):
                n = ROUND * i + j
                if not no_weights:
                    c, par, loads = next_chunk(i, j)
                    unpack(c, par, j % TC, loads)
                    lo_weights(c, par, j % TC)
                if not final:
                    elementwise(n + 1, (j + 1) % 2)
                dve.wait_ge(down_done, n + 3)
                here = acc[:, :, (j % TC) * W:(j % TC + 1) * W]
                nc.vector.tensor_tensor(here, here, p_out[:, :, :], ALU.add).then_inc(added, 1)

            dve.sem_inc(gelu_done, 1)
            dve.sem_inc(i_lo_done, 1)
            dve.sem_inc(inter_done, 1)
            dve.sem_inc(added, 1)
            for m in range(3):
                unpack(0, 0, m, 1, first=True)
                lo_weights(0, 0, m)
            elementwise(0, 0)
            steps(dve, body)

        @block.tensor
        def _(pe):
            def gate_and_up(i, j, n):
                par = j // TC % 2
                tokens = slice((j % TC) * W, (j % TC + 1) * W)
                for m, bank, free, done in ((0, p_gate, gate_out, gate_done), (1, p_up, inter_done, up_done)):
                    if j % TC == 0:
                        pe.wait_ge(weight_lo, 3 * (PAIR * i + j // TC) + m + 1)
                    pe.wait_ge(free, 2 * n + 2 if m == 0 else n + 1)
                    for nt in range(2):
                        for kt in range(KT):
                            rows = slice((kt % 2) * CN + nt * P, (kt % 2) * CN + (nt + 1) * P)
                            last = mm3(nc, bank[:, nt, :], w_hi[par][:, m, kt // 2, rows],
                                       w_lo[par][:, m, kt // 2, rows], xn_hi[:, kt, tokens], xn_lo[:, kt, tokens],
                                       kt == 0, kt == KT - 1)
                    last.then_inc(done, 1)

            def down(i, j, n):
                par = j // TC % 2
                if j % TC == 0:
                    pe.wait_ge(weight_lo, 3 * (PAIR * i + j // TC) + 3)
                pe.wait_ge(i_lo_done, n + 2)
                pe.wait_ge(added, n + 1)
                for ot in range(KT):
                    for nt in range(2):
                        last = mm3(nc, p_out[:, ot, :], w_hi[par][:, 2, nt, ot * P:(ot + 1) * P],
                                   w_lo[par][:, 2, nt, ot * P:(ot + 1) * P], i_hi[:, j % 2, nt, :],
                                   i_lo[:, j % 2, nt, :], nt == 0, nt == 1)
                last.then_inc(down_done, 1)

            def body(i, j, final, no_weights):
                n = ROUND * i + j
                if not final:
                    ni, nj = (i + 1, 0) if j == ROUND - 1 else (i, j + 1)
                    gate_and_up(ni, nj, n + 1)
                down(i, j, n)

            pe.sem_inc(up_done, 1)
            pe.sem_inc(down_done, 2)
            gate_and_up(0, 0, 0)
            steps(pe, body)


def layer(nc, x, x_t, wqkv_t, wo_t, gate_p, up_p, gate_up_s, down_p, down_s, out_t):
    qk_scratch = nc.dram_tensor("qk_scratch", (2, 2, H, S), F32).ap()
    v_scratch = nc.dram_tensor("v_scratch", (S, 2 * NH, D), F32).ap()
    sum_scratch = nc.dram_tensor("sum_scratch", (NH, S), F32).ap()
    rsum_scratch = nc.dram_tensor("rsum_scratch", (NH, S), F32).ap()
    with nc.sbuf_tensor("xn_hi", [P, KT, S], F32R) as xn_hi, nc.sbuf_tensor("xn_lo", [P, KT, S], F32R) as xn_lo:
        norm_and_project(nc, x, wqkv_t, qk_scratch, v_scratch, xn_hi, xn_lo)
        with nc.sbuf_tensor("acc", [P, KT * S], F32) as acc:
            attention(nc, qk_scratch, v_scratch, sum_scratch, acc)
            output_projection(nc, x_t, wo_t, sum_scratch, rsum_scratch, acc)
            feed_forward(nc, gate_p, up_p, gate_up_s, down_p, down_s, xn_hi, xn_lo, acc, out_t)


def kernel(**inputs):
    import numpy as _np
    import concourse.bacc as _bacc
    from concourse import mybir as _mybir
    from concourse.bass_utils import run_bass_kernel_spmd as _run

    a = {k[3:]: _np.asarray(v) for k, v in inputs.items()}
    x = a["attn_hidden_states"].reshape(S, H)

    def by_tiles(w):
        return w.reshape(MLP // (2 * P), P, 2, -1).transpose(3, 0, 2, 1).reshape(w.shape[1], MLP)

    laid = {
        "x": x,
        "x_t": x.T,
        "wqkv_t": a["attn_w_qkv"].T.reshape(H // 2, 2, 3 * H).transpose(1, 0, 2).reshape(H, 3 * H),
        "wo_t": a["attn_w_o"].T,
        "gate_p": by_tiles(a["ffn_gate_W_packed"]),
        "up_p": by_tiles(a["ffn_up_W_packed"]),
        "gate_up_s": _np.stack([by_tiles(a["ffn_gate_scales"]), by_tiles(a["ffn_up_scales"])])
        .reshape(2, 2, H // 64, MLP),
        "down_p": a["ffn_down_W_packed"].T,
        "down_s": a["ffn_down_scales"].T,
    }
    nc = _bacc.Bacc("TRN2", target_bir_lowering=False, num_devices=1)
    arrays, args = {}, []
    for name, v in laid.items():
        v = _np.ascontiguousarray(v)
        arrays[f"in_{name}"] = v
        args.append(nc.dram_tensor(f"in_{name}", v.shape, _mybir.dt.from_np(v.dtype), kind="ExternalInput").ap())
    args.append(nc.dram_tensor("out_t", (H, S), _mybir.dt.float32, kind="ExternalOutput").ap())
    layer(nc, *args)
    r = _run(nc, [arrays], core_ids=[0])
    return _np.ascontiguousarray(r.results[0]["out_t"].T).reshape(1, S, H)
```

```python
import numpy as np
import concourse.bass as bass
from concourse import mybir
from contextlib import ExitStack

F32 = mybir.dt.float32
F32R = mybir.dt.float32r
BF16 = mybir.dt.bfloat16
F16 = mybir.dt.float16
I32 = mybir.dt.int32
ALU = mybir.AluOpType
ACT = mybir.ActivationFunctionType
AX = mybir.AxisListType

P = 128
S = 2048
H = 512
NH = 16
D = H // NH
MLP = 4096
KT = H // P
TT = S // P
W = 512
TC = S // W
EPS = 1e-5
MASKED = -float(2 ** 100)
NO_MAX = -3.0e38
SCALE = 1.0 / float(np.sqrt(np.float32(D)))


def mm3(nc, out, w_hi, w_lo, x_hi, x_lo, first, last):
    nc.tensor.matmul(out, w_hi, x_hi, start=first, stop=False)
    nc.tensor.matmul(out, w_hi, x_lo, start=False, stop=False)
    return nc.tensor.matmul(out, w_lo, x_hi, start=False, stop=last)


def norm_and_project(nc, x, wqkv_t, qk_scratch, v_scratch, xn_lo_scratch, xn_hi, xn_lo):
    LOADS = 4
    PER = TT // LOADS
    UNITS_QK = 2 * KT * TC
    UNITS = UNITS_QK + TT
    SLOTS = 4
    with ExitStack() as ctx:
        def sb(name, shape, dt):
            return ctx.enter_context(nc.sbuf_tensor(name, shape, dt))

        def sem(name):
            return ctx.enter_context(nc.semaphore(name))

        x_sb = sb("x_sb", [P, TT, H], F32)
        w_sb = sb("wqkv_sb", [P, KT, 3 * H], F32)
        w_hi = sb("wqkv_hi", [P, KT, 3 * H], F32R)
        w_lo = sb("wqkv_lo", [P, KT, 3 * H], F32R)
        ident = sb("ident1", [P, P], F32)
        stats = sb("stats", [P, TT, 6], F32)
        mean_var = sb("mean_var", [P, TT, 2], F32)
        var_eps = sb("var_eps", [P, TT], F32)
        std = sb("std", [P, TT], F32)
        rstd = sb("rstd", [P, TT], F32)
        out_hi = sb("out_hi", [P, SLOTS, W], F32R)
        out_lo = sb("out_lo", [P, SLOTS, W], F32R)
        out_v = sb("out_v", [P, 2, NH, 2, D], F32R)
        pt = ctx.enter_context(nc.psum_tensor("pt", [P, 2, W], F32))
        pj = ctx.enter_context(nc.psum_tensor("pj", [P, SLOTS, W], F32))

        x_loaded = [sem(f"x_loaded{i}") for i in range(LOADS)]
        w_loaded = [sem(f"w_loaded{i}") for i in range(3)]
        ident_made = sem("ident_made")
        stats_made = sem("stats_made")
        std_made = sem("std_made")
        rstd_made = sem("rstd_made")
        xn_made = sem("xn_made")
        transposed = sem("transposed")
        xn_hi_made = sem("xn_hi_made")
        xn_lo_made = sem("xn_lo_made")
        xn_lo_stored = sem("xn_lo_stored")
        w_hi_made = sem("w_hi_made")
        w_lo_made = sem("w_lo_made")
        projected = sem("projected")
        hi_made = sem("hi_made")
        lo_made = sem("lo_made")
        stored = [sem(f"stored{i}") for i in range(SLOTS)]
        stored_v = [sem(f"stored_v{i}") for i in range(2)]
        block = ctx.enter_context(nc.Block())

        @block.sync
        def _(sp):
            for i in range(LOADS):
                sp.dma_start(x_sb[:, i * PER:(i + 1) * PER, :],
                             x[i * PER * P:(i + 1) * PER * P, :].rearrange("(t p) h -> p t h", p=P)
                             ).then_inc(x_loaded[i], 16)
                if i < 3:
                    sp.dma_start(w_sb[:, :, i * H:(i + 1) * H],
                                 wqkv_t[:, i * H:(i + 1) * H].rearrange("(k p) o -> p k o", p=P)
                                 ).then_inc(w_loaded[i], 16)
            sp.wait_ge(xn_lo_made, TT)
            sp.dma_start(xn_lo_scratch, xn_lo[:, :, :].bitcast(F32)).then_inc(xn_lo_stored, 16)
            for u in range(UNITS):
                sp.wait_ge(hi_made, u + 1)
                sp.wait_ge(lo_made, u + 1)
                if u < UNITS_QK:
                    ot, tc = divmod(u, TC)
                    rows = slice((ot % KT) * P, (ot % KT + 1) * P)
                    for part, tile in ((0, out_hi), (1, out_lo)):
                        sp.dma_start(qk_scratch[ot // KT, part, rows, tc * W:(tc + 1) * W],
                                     tile[:, u % SLOTS, :].bitcast(F32)).then_inc(stored[u % SLOTS], 16)
                else:
                    tt = u - UNITS_QK
                    sp.dma_start(v_scratch[tt * P:(tt + 1) * P, :, :],
                                 out_v[:, tt % 2, :, :, :].rearrange("p h a d -> p h (a d)").bitcast(F32)
                                 ).then_inc(stored_v[tt % 2], 16)
            sp.wait_ge(xn_lo_stored, 16)
            for s in range(SLOTS):
                sp.wait_ge(stored[s], 32 * (UNITS_QK // SLOTS))
            for s in range(2):
                sp.wait_ge(stored_v[s], 16 * (TT // 2))

        @block.gpsimd
        def _(pool):
            nc.gpsimd.memset(ident[:, :], 0.0).then_inc(ident_made, 1)
            pool.wait_ge(ident_made, 1)
            nc.gpsimd.affine_select(out=ident[:, :], in_=ident[:, :], compare_op=ALU.not_equal, fill=1.0,
                                    base=0, pattern=[[-1, P]], channel_multiplier=1).then_inc(ident_made, 1)

        @block.scalar
        def _(act):
            for i in range(LOADS):
                act.wait_ge(stats_made, (2 * PER + 1) * (i + 1))
                cols = slice(i * PER, (i + 1) * PER)
                nc.scalar.activation(std[:, cols], var_eps[:, cols], ACT.Sqrt).then_inc(std_made, 1)
            for i in range(3):
                act.wait_ge(w_loaded[i], 16)
                nc.scalar.activation(w_hi[:, :, i * H:(i + 1) * H], w_sb[:, :, i * H:(i + 1) * H],
                                     ACT.Copy).then_inc(w_hi_made, 1)
            for tt in range(TT):
                act.wait_ge(transposed, tt + 1)
                nc.scalar.activation(xn_hi[:, :, tt * P:(tt + 1) * P],
                                     pt[:, tt % 2, :].rearrange("p (k t) -> p k t", k=KT),
                                     ACT.Copy).then_inc(xn_hi_made, 1)
            for u in range(UNITS):
                act.wait_ge(projected, u + 1)
                if u < UNITS_QK:
                    if u >= SLOTS:
                        act.wait_ge(stored[u % SLOTS], 32 * (u // SLOTS))
                    nc.scalar.activation(out_hi[:, u % SLOTS, :], pj[:, u % SLOTS, :],
                                         ACT.Copy).then_inc(hi_made, 1)
                else:
                    tt = u - UNITS_QK
                    if tt >= 2:
                        act.wait_ge(stored_v[tt % 2], 16 * (tt // 2))
                    nc.scalar.activation(out_v[:, tt % 2, :, 0, :],
                                         pj[:, u % SLOTS, :].rearrange("p (h d) -> p h d", h=NH),
                                         ACT.Copy).then_inc(hi_made, 1)

        @block.vector
        def _(dve):
            n = 0
            for i in range(LOADS):
                dve.wait_ge(x_loaded[i], 16)
                for tt in range(i * PER, (i + 1) * PER):
                    nc.vector.bn_stats(stats[:, tt, :], x_sb[:, tt, :]).then_inc(stats_made, 1)
                n += PER
                for tt in range(i * PER, (i + 1) * PER):
                    dve.wait_ge(stats_made, n)
                    nc.vector.bn_aggr(mean_var[:, tt, :], stats[:, tt, :])\
                        .then_inc(stats_made, 1)
                    n += 1
                dve.wait_ge(stats_made, n)
                cols = slice(i * PER, (i + 1) * PER)
                nc.vector.tensor_scalar(var_eps[:, cols], mean_var[:, cols, 1], EPS, None,
                                        ALU.add).then_inc(stats_made, 1)
                n += 1
                dve.wait_ge(std_made, i + 1)
                nc.vector.reciprocal(rstd[:, cols], std[:, cols]).then_inc(rstd_made, 1)
                dve.wait_ge(rstd_made, i + 1)
                for tt in range(i * PER, (i + 1) * PER):
                    nc.vector.tensor_scalar(x_sb[:, tt, :], x_sb[:, tt, :], mean_var[:, tt, 0:1],
                                            rstd[:, tt:tt + 1], ALU.subtract, ALU.mult).then_inc(xn_made, 1)
            for tt in range(TT):
                dve.wait_ge(xn_hi_made, tt + 1)
                cols = slice(tt * P, (tt + 1) * P)
                nc.vector.tensor_tensor(xn_lo[:, :, cols], pt[:, tt % 2, :].rearrange("p (k t) -> p k t", k=KT),
                                        xn_hi[:, :, cols].bitcast(F32), ALU.subtract).then_inc(xn_lo_made, 1)
                if tt % 4 == 3 and tt // 4 < 3:
                    i = tt // 4
                    dve.wait_ge(w_hi_made, i + 1)
                    cols = slice(i * H, (i + 1) * H)
                    nc.vector.tensor_tensor(w_lo[:, :, cols], w_sb[:, :, cols], w_hi[:, :, cols].bitcast(F32),
                                            ALU.subtract).then_inc(w_lo_made, 1)
            for u in range(UNITS):
                dve.wait_ge(hi_made, u + 1)
                if u < UNITS_QK:
                    nc.vector.tensor_tensor(out_lo[:, u % SLOTS, :], pj[:, u % SLOTS, :],
                                            out_hi[:, u % SLOTS, :].bitcast(F32), ALU.subtract).then_inc(lo_made, 1)
                else:
                    tt = u - UNITS_QK
                    nc.vector.tensor_tensor(out_v[:, tt % 2, :, 1, :],
                                            pj[:, u % SLOTS, :].rearrange("p (h d) -> p h d", h=NH),
                                            out_v[:, tt % 2, :, 0, :].bitcast(F32), ALU.subtract).then_inc(lo_made, 1)

        @block.tensor
        def _(pe):
            pe.wait_ge(ident_made, 2)
            for tt in range(TT):
                pe.wait_ge(xn_made, tt + 1)
                if tt >= 2:
                    pe.wait_ge(xn_lo_made, tt - 1)
                for kt in range(KT):
                    par, half = divmod(kt, 2)
                    first = 2 * P * half + par
                    last = nc.tensor.transpose(pt[:, tt % 2, kt * P:(kt + 1) * P],
                                               x_sb[:, tt, first:first + 2 * P - 1:2], ident[:, :])
                last.then_inc(transposed, 1)
            pe.wait_ge(xn_lo_made, TT)
            for u in range(UNITS):
                if u % (KT * TC) == 0:
                    pe.wait_ge(w_lo_made, u // (KT * TC) + 1)
                if u >= SLOTS:
                    pe.wait_ge(lo_made, u - SLOTS + 1)
                for kt in range(KT):
                    if u < UNITS_QK:
                        ot, tc = divmod(u, TC)
                        o, t = slice(ot * P, (ot + 1) * P), slice(tc * W, (tc + 1) * W)
                        last = mm3(nc, pj[:, u % SLOTS, :], w_hi[:, kt, o], w_lo[:, kt, o],
                                   xn_hi[:, kt, t], xn_lo[:, kt, t], kt == 0, kt == KT - 1)
                    else:
                        tt = u - UNITS_QK
                        o, t = slice(2 * H, 3 * H), slice(tt * P, (tt + 1) * P)
                        last = mm3(nc, pj[:, u % SLOTS, :], xn_hi[:, kt, t], xn_lo[:, kt, t],
                                   w_hi[:, kt, o], w_lo[:, kt, o], kt == 0, kt == KT - 1)
                last.then_inc(projected, 1)


def attention(nc, qk_scratch, v_scratch, sum_scratch, attn_t):
    GROUP = 4
    ROWS = 3 * D
    VW = 3 * D
    CAP = W
    QK_BUFS = GROUP
    V_BUFS = 2
    E_BUFS = 4
    LO_LEAD = 1
    HI_LEAD = 2
    LEAD = 3
    UNITS = [(i, k, min(CAP, P * (i + 1) - k)) for i in range(TT) for k in range(0, P * (i + 1), CAP)]
    NU = len(UNITS)
    STEPS = [(qc, pair, 0 if pair < 2 * qc + 1 else W // 2) for qc in range(TC) for pair in range(2 * qc + 2)]
    NS = len(STEPS)
    WHOLE = {8, 13, 17}
    POOL_HI = set(range(NS))
    POOL_LO = {3, 6, 11, 16}
    LAST = [s for s in range(NS) if s + 1 == NS or STEPS[s + 1][0] != STEPS[s][0]]
    CHAIN = 3 * NS // 4
    BESIDE = {s: [] for s in range(NS)}
    for u in range(NU):
        ahead, s = divmod(CHAIN + u * NS // NU, NS)
        BESIDE[s].append((2 - ahead, u))
    HI = [None if s in WHOLE else "pool" if s in POOL_HI else "act" for s in range(NS)]
    LO = [None if s in WHOLE else "pool" if s in POOL_LO else "dve" for s in range(NS)]
    CREDIT = 4

    def made(parts, who, h, s):
        whole, part = divmod(s, NS)
        return (h + whole) * parts.count(who) + parts[:part + 1].count(who) + CREDIT

    with ExitStack() as ctx:
        def sb(name, shape, dt):
            return ctx.enter_context(nc.sbuf_tensor(name, shape, dt))

        def sem(name):
            return ctx.enter_context(nc.semaphore(name))

        q_stack = [sb(f"q_stack{i}", [P, S], F32R) for i in range(QK_BUFS)]
        k_stack = [sb(f"k_stack{i}", [P, S], F32R) for i in range(QK_BUFS)]
        v_stack = [sb(f"v_stack{i}", [P, TT, VW], F32R) for i in range(V_BUFS)]
        e_sb = sb("e_sb", [P, E_BUFS, 2, W], F32)
        e_hi = sb("e_hi", [P, E_BUFS, 2, W], F32R)
        e_lo = sb("e_lo", [P, E_BUFS, 2, W], F32R)
        lo_sum = sb("lo_sum", [D + 1, 2, W], F32)
        max_part = sb("max_part", [P, TT, TC], F32)
        row_max = sb("row_max", [P, TT], F32)
        rest1 = sb("rest1", [P, TT], F32)
        rest2 = sb("rest2", [P, TT], F32)
        max_cols = sb("max_cols", [P, TT, P], BF16)
        ident = sb("ident_bf", [P, P], BF16)
        mask_q = sb("mask_q", [P, P], BF16)
        mask_k = sb("mask_k", [P, 2 * P], BF16)
        p_st = ctx.enter_context(nc.psum_tensor("p_st", [P, 2, 2, W], F32))
        p_s = ctx.enter_context(nc.psum_tensor("p_s", [P, 2, W], F32))
        p_o = ctx.enter_context(nc.psum_tensor("p_o", [P, 2, W], F32))

        consts = sem("consts")
        minus_one = sem("minus_one")
        pool_turns = sem("pool_turns_attn")
        qk_loaded = [sem(f"qk_loaded{i}") for i in range(QK_BUFS)]
        v_loaded = [sem(f"v_loaded{i}") for i in range(V_BUFS)]
        scored = sem("scored")
        maxed = sem("maxed")
        max_step = sem("max_step")
        max_split = sem("max_split")
        max_turned = sem("max_turned")
        max_rows = sem("max_rows")
        st_ready = sem("st_ready")
        exp_done = sem("exp_done")
        hi_made = {who: sem(f"e_hi_made_{who}") for who in ("act", "pool")}
        lo_made = {who: sem(f"e_lo_made_{who}") for who in ("dve", "pool")}
        pv_done = sem("pv_done")
        lo_sum_made = sem("lo_sum_made")
        o_free = sem("o_free")
        sums_out = [sem(f"sums_out{i}") for i in range(2)]
        block = ctx.enter_context(nc.Block())
        NC = 6

        def load_qk(sp, h, par):
            rows = bass.ds(h * D, D)
            for strip, part in enumerate((0, 0, 1)):
                sp.dma_start(q_stack[par][strip * D:(strip + 1) * D, :].bitcast(F32),
                             qk_scratch[0, part, rows, :]).then_inc(qk_loaded[par], 16)
            for strip, part in enumerate((0, 1, 0)):
                sp.dma_start(k_stack[par][strip * D:(strip + 1) * D, :].bitcast(F32),
                             qk_scratch[1, part, rows, :]).then_inc(qk_loaded[par], 16)

        def load_v(sp, h, par):
            for part, col in ((0, 2 * D), (1, 0)):
                sp.dma_start(v_stack[par][:, :, col:col + D].bitcast(F32),
                             v_scratch[:, bass.ds(2 * h + part, 1), :].rearrange("(t p) a d -> p t (a d)", p=P)
                             ).then_inc(v_loaded[par], 16)

        @block.sync
        def _(sp):
            load_qk(sp, 0, 0)
            load_v(sp, 0, 0)
            for h in range(1, QK_BUFS - 1):
                load_qk(sp, h, h)

            def group(g, last):
                for j in range(GROUP):
                    h = g * GROUP + j
                    sp.wait_ge(pv_done, h * NS + E_BUFS)
                    if not (last and j + 1 >= GROUP):
                        load_v(sp, h + 1, (j + 1) % V_BUFS)
                    if not (last and j + QK_BUFS - 1 >= GROUP):
                        load_qk(sp, h + QK_BUFS - 1, (j + QK_BUFS - 1) % QK_BUFS)
                    for qc in range(TC):
                        sp.wait_ge(lo_sum_made, h * TC + qc + 1)
                        sp.dma_start(sum_scratch[bass.ds(h, 1), qc * W:(qc + 1) * W],
                                     lo_sum[D:D + 1, qc % 2, :]).then_inc(sums_out[qc % 2], 16)

            sp.sem_inc(sums_out[0], 16)
            sp.sem_inc(sums_out[1], 16)
            with sp.Fori(0, NH // GROUP - 1) as g:
                group(g, False)
            group(NH // GROUP - 1, True)
            for s in sums_out:
                sp.wait_ge(s, 16 * (NH * TC // 2 + 1))

        def ahead(g, j, s, steps, last):
            dj, s = divmod(s + steps, NS)
            if last and j + dj >= GROUP:
                return None
            return g * GROUP + j + dj, (j + dj) % GROUP, s

        def make_hi(eng, h, s):
            who, n, w = HI[s], h * NS + s, W - STEPS[s][2]
            eng.wait_ge(exp_done, n + 3)
            eng.wait_ge(pv_done, n + 1)
            if who == "act":
                nc.scalar.activation(e_hi[:, s % E_BUFS, :, 0:w], e_sb[:, s % E_BUFS, :, 0:w],
                                     ACT.Copy).then_inc(hi_made["act"], 1)
            else:
                eng.sem_inc(pool_turns, 1)
                nc.gpsimd.tensor_scalar(e_hi[:, s % E_BUFS, :, 0:w], e_sb[:, s % E_BUFS, :, 0:w], 1.0, 1.0, ALU.mult,
                                        ALU.mult).then_inc(hi_made["pool"], 1)

        def make_lo(eng, h, s):
            who, w = LO[s], W - STEPS[s][2]
            eng.wait_ge(hi_made[HI[s]], made(HI, HI[s], h, s))
            eng.wait_ge(pv_done, h * NS + s + 1)
            engine = nc.gpsimd if who == "pool" else nc.vector
            engine.tensor_tensor(e_lo[:, s % E_BUFS, :, 0:w], e_sb[:, s % E_BUFS, :, 0:w],
                                 e_hi[:, s % E_BUFS, :, 0:w].bitcast(F32), ALU.subtract).then_inc(lo_made[who], 1)

        @block.gpsimd
        def _(pool):
            nc.gpsimd.memset(ident[:, :], 0.0).then_inc(consts, 1)
            nc.gpsimd.memset(mask_q[:, :], 0.0).then_inc(consts, 1)
            nc.gpsimd.memset(mask_k[:, 0:P], MASKED).then_inc(consts, 1)
            nc.gpsimd.memset(mask_k[:, P:], 0.0).then_inc(consts, 1)
            nc.gpsimd.memset(max_cols[:, :, :], 0.0).then_inc(consts, 1)
            nc.gpsimd.memset(max_part[:, :, :], NO_MAX).then_inc(consts, 1)
            pool.wait_ge(consts, NC)
            nc.gpsimd.affine_select(out=ident[:, :], in_=ident[:, :], compare_op=ALU.not_equal, fill=1.0,
                                    base=0, pattern=[[-1, P]], channel_multiplier=1).then_inc(consts, 1)
            nc.gpsimd.affine_select(out=mask_q[:, :], in_=mask_q[:, :], compare_op=ALU.is_ge, fill=MASKED,
                                    base=0, pattern=[[-1, P]], channel_multiplier=1).then_inc(consts, 1)
            nc.gpsimd.affine_select(out=mask_k[:, P:], in_=mask_k[:, P:], compare_op=ALU.is_ge, fill=MASKED,
                                    base=0, pattern=[[1, P]], channel_multiplier=-1).then_inc(consts, 1)
            pool.wait_ge(consts, NC + 3)
            pool.sem_inc(hi_made["pool"], CREDIT)
            pool.sem_inc(lo_made["pool"], CREDIT)

            def hi(h, s):
                if HI[s] == "pool":
                    make_hi(pool, h, s)

            def lo(h, s):
                if LO[s] == "pool":
                    make_lo(pool, h, s)

            def group(g, last):
                for j in range(GROUP):
                    for s in range(NS):
                        if (at := ahead(g, j, s, HI_LEAD, last)) is not None:
                            hi(at[0], at[2])
                        if (at := ahead(g, j, s, LO_LEAD, last)) is not None:
                            lo(at[0], at[2])

            for s in range(HI_LEAD):
                hi(0, s)
            for s in range(LO_LEAD):
                lo(0, s)
            with pool.Fori(0, NH // GROUP - 1) as g:
                group(g, False)
            group(NH // GROUP - 1, True)

        @block.scalar
        def _(act):
            def max_row(h, par, r):
                act.wait_ge(max_turned, h * TC + r + 1)
                nc.scalar.activation(q_stack[par][ROWS:P, r * W:(r + 1) * W], p_o[ROWS:P, 0, :],
                                     ACT.Copy).then_inc(max_rows, 1)

            def exps(h, s):
                qc, pair, q0 = STEPS[s]
                w = W - q0
                act.wait_ge(st_ready, h * NS + s + 1)
                before = s - E_BUFS
                if before % NS in WHOLE:
                    act.wait_ge(pv_done, h * NS + s + 1)
                else:
                    act.wait_ge(lo_made[LO[before]], made(LO, LO[before], h, before))
                nc.scalar.activation(e_sb[:, s % E_BUFS, :, 0:w], p_st[:, s % 2, :, 0:w], ACT.Exp,
                                     scale=SCALE).then_inc(exp_done, 1)

            def lower_part(h, s):
                qc = STEPS[s][0]
                act.wait_ge(pv_done, h * NS + s + 1 + E_BUFS)
                act.wait_ge(sums_out[qc % 2], (h * 2 + qc // 2 + 1) * 16)
                nc.scalar.activation(lo_sum[:, qc % 2, :], p_o[0:D + 1, qc % 2, :],
                                     ACT.Copy).then_inc(lo_sum_made, 1)

            act.sem_inc(exp_done, 2)
            act.sem_inc(hi_made["act"], CREDIT)
            for r in range(TC):
                max_row(0, 0, r)
            for s in range(LEAD):
                exps(0, s)
                if s < LEAD - 1 and HI[s] == "act":
                    make_hi(act, 0, s)

            def group(g, last):
                for j in range(GROUP):
                    h = g * GROUP + j
                    final = last and j == GROUP - 1
                    for s in range(NS):
                        if (at := ahead(g, j, s, LEAD - 1, last)) is not None and HI[at[2]] == "act":
                            make_hi(act, at[0], at[2])
                        if (at := ahead(g, j, s, LEAD, last)) is not None:
                            exps(at[0], at[2])
                        if s >= NS - TC and not final:
                            max_row(h + 1, (j + 1) % QK_BUFS, s - (NS - TC))
                        if s - 1 in LAST:
                            lower_part(h, s - 1)
                    lower_part(h, NS - 1)

            with act.Fori(0, NH // GROUP - 1) as g:
                group(g, False)
            group(NH // GROUP - 1, True)

        @block.vector
        def _(dve):
            for k in k_stack:
                nc.vector.memset(k[ROWS:P, :].bitcast(F32), 0.0).then_inc(minus_one, 1)
            for v in v_stack:
                nc.vector.memset(v[:, :, D:2 * D].bitcast(F32), 0.0).then_inc(minus_one, 1)
            dve.wait_ge(minus_one, QK_BUFS + V_BUFS)
            for k in k_stack:
                nc.vector.memset(k[ROWS:ROWS + 3, :].bitcast(F32), -1.0).then_inc(minus_one, 1)
            for v in v_stack:
                nc.vector.memset(v[:, :, D:D + 1].bitcast(F32), 1.0).then_inc(minus_one, 1)
            dve.wait_ge(consts, NC)
            dve.sem_inc(lo_made["dve"], CREDIT)
            dve.sem_inc(o_free, 2)

            def unit_max(h, u):
                i, k, w = UNITS[u]
                dve.wait_ge(scored, h * NU + u + 1)
                nc.vector.reduce_max(max_part[:, i, k // CAP:k // CAP + 1],
                                     p_s[:, u % 2, 0:w], AX.X).then_inc(maxed, 1)

            def split_max(h, first=False):
                dve.wait_ge(maxed, (h + 1) * NU + 2)
                if not first:
                    dve.wait_ge(max_turned, h * TC)
                nc.vector.reduce_max(row_max[:, :], max_part[:, :, :], AX.X).then_inc(max_step, 1)
                dve.wait_ge(max_step, h * 5 + 1)
                nc.vector.tensor_copy(max_cols[:, :, ROWS], row_max[:, :]).then_inc(max_step, 1)
                dve.wait_ge(max_step, h * 5 + 2)
                nc.vector.tensor_tensor(rest1[:, :], row_max[:, :], max_cols[:, :, ROWS],
                                        ALU.subtract).then_inc(max_step, 1)
                dve.wait_ge(max_step, h * 5 + 3)
                nc.vector.tensor_copy(max_cols[:, :, ROWS + 1], rest1[:, :]).then_inc(max_step, 1)
                dve.wait_ge(max_step, h * 5 + 4)
                nc.vector.tensor_tensor(rest2[:, :], rest1[:, :], max_cols[:, :, ROWS + 1],
                                        ALU.subtract).then_inc(max_step, 1)
                dve.wait_ge(max_step, h * 5 + 5)
                nc.vector.tensor_copy(max_cols[:, :, ROWS + 2], rest2[:, :]).then_inc(max_split, 1)

            def add_parts(g, h, j, qc):
                dve.wait_ge(lo_sum_made, h * TC + qc + 1)
                nc.vector.tensor_tensor(attn_t[j * D:(j + 1) * D, bass.ds(g * S + qc * W, W)],
                                        p_o[2 * D:VW, qc % 2, :], lo_sum[0:D, qc % 2, :],
                                        ALU.add).then_inc(o_free, 1)

            for u in range(NU):
                unit_max(0, u)
            split_max(0, first=True)
            for s in range(CHAIN, NS):
                for heads, u in BESIDE[s]:
                    unit_max(heads - 1, u)
            for s in range(LO_LEAD):
                if LO[s] == "dve":
                    make_lo(dve, 0, s)

            def group(g, last):
                for j in range(GROUP):
                    h = g * GROUP + j
                    for s in range(NS):
                        if s == CHAIN and not (last and j + 1 >= GROUP):
                            split_max(h + 1)
                        if (at := ahead(g, j, s, LO_LEAD, last)) is not None and LO[at[2]] == "dve":
                            make_lo(dve, at[0], at[2])
                        for heads, u in BESIDE[s]:
                            if not (last and j + heads >= GROUP):
                                unit_max(h + heads, u)
                        if s - 1 in LAST:
                            add_parts(g, h, j, STEPS[s - 1][0])
                    add_parts(g, h, j, TC - 1)

            with dve.Fori(0, NH // GROUP - 1) as g:
                group(g, False)
            group(NH // GROUP - 1, True)

        @block.tensor
        def _(pe):
            pe.sem_inc(pv_done, E_BUFS)
            pe.wait_ge(consts, NC + 3)
            pe.wait_ge(minus_one, 2 * (QK_BUFS + V_BUFS))

            def scores(h, par, u):
                i, k, w = UNITS[u]
                diagonal = k + w == P * (i + 1)
                pe.wait_ge(maxed, h * NU + u + 1)
                last = nc.tensor.matmul(p_s[:, u % 2, 0:w], q_stack[par][0:ROWS, i * P:(i + 1) * P],
                                        k_stack[par][0:ROWS, k:k + w], start=True, stop=not diagonal)
                if diagonal:
                    last = nc.tensor.matmul(p_s[:, u % 2, w - P:w], ident[:, :], mask_q[:, :],
                                            start=False, stop=True)
                last.then_inc(scored, 1)

            def turn_max(h, r):
                if r == 0:
                    pe.wait_ge(max_split, h + 1)
                    pe.wait_ge(o_free, h * TC + 1)
                pe.wait_ge(max_rows, h * TC + r + 1)
                for t in range(W // P):
                    last = nc.tensor.matmul(p_o[:, 0, t * P:(t + 1) * P], max_cols[:, r * (W // P) + t, :],
                                            ident[:, :], start=True, stop=True)
                last.then_inc(max_turned, 1)

            def scores_t(h, par, s):
                qc, pair, q0 = STEPS[s]
                w = W - q0
                if pair == 0:
                    pe.wait_ge(max_rows, h * TC + qc + 2)
                pe.wait_ge(exp_done, h * NS + s + 1)
                for t in range(2):
                    kt = 2 * pair + t
                    diagonal = kt * P >= qc * W
                    last = nc.tensor.matmul(p_st[:, s % 2, t, 0:w], k_stack[par][:, kt * P:(kt + 1) * P],
                                            q_stack[par][:, qc * W + q0:(qc + 1) * W], start=True,
                                            stop=not diagonal)
                    if diagonal:
                        last = nc.tensor.matmul(p_st[:, s % 2, t, 0:(t + 1) * P], ident[:, :],
                                                mask_k[:, (1 - t) * P:], start=False, stop=True)
                last.then_inc(st_ready, 1)

            def product_v(h, par, s):
                qc, pair, q0 = STEPS[s]
                w = W - q0
                if pair == 0:
                    pe.wait_ge(o_free, h * TC + qc + 1)
                if s == 0:
                    pe.wait_ge(max_rows, (h + 1) * TC + 1)
                final_step = s in LAST
                if s in WHOLE:
                    pe.wait_ge(exp_done, h * NS + s + 3)
                    for t in range(2):
                        last = nc.tensor.matmul(p_o[0:VW, qc % 2, q0:], v_stack[par][:, 2 * pair + t, :].bitcast(F32),
                                                e_sb[:, s % E_BUFS, t, 0:w], start=(pair == 0 and t == 0),
                                                stop=(final_step and t == 1))
                    last.then_inc(pv_done, 1)
                    return
                pe.wait_ge(hi_made[HI[s]], made(HI, HI[s], h, s))
                for part, tile in ((0, e_hi), (1, e_lo)):
                    if part:
                        pe.wait_ge(lo_made[LO[s]], made(LO, LO[s], h, s))
                    for t in range(2):
                        last = nc.tensor.matmul(p_o[0:VW, qc % 2, q0:], v_stack[par][:, 2 * pair + t, :],
                                                tile[:, s % E_BUFS, t, 0:w], start=(pair == 0 and part == 0 and t == 0),
                                                stop=(final_step and part == 1 and t == 1))
                last.then_inc(pv_done, 1)

            pe.sem_inc(maxed, 2)
            pe.sem_inc(max_rows, 1)
            for u in range(NU):
                if u == 0:
                    pe.wait_ge(qk_loaded[0], 96)
                scores(0, 0, u)
            for r in range(TC):
                turn_max(0, r)
            for s in range(LEAD):
                scores_t(0, 0, s)
            for s in range(CHAIN, NS):
                for heads, u in BESIDE[s]:
                    if u == 0:
                        pe.wait_ge(qk_loaded[heads - 1], 96)
                    scores(heads - 1, heads - 1, u)

            def group(g, last):
                for j in range(GROUP):
                    h = g * GROUP + j
                    pe.wait_ge(v_loaded[j % V_BUFS], (g * (GROUP // V_BUFS) + j // V_BUFS + 1) * 32)
                    for s in range(NS):
                        if (at := ahead(g, j, s, LEAD, last)) is not None:
                            scores_t(*at)
                        for heads, u in BESIDE[s]:
                            if last and j + heads >= GROUP:
                                continue
                            par = (j + heads) % QK_BUFS
                            if u == 0:
                                pe.wait_ge(qk_loaded[par], (g + (j + heads) // QK_BUFS + 1) * 96)
                            scores(h + heads, par, u)
                        if s >= NS - TC and not (last and j + 1 >= GROUP):
                            turn_max(h + 1, s - (NS - TC))
                        product_v(h, j % V_BUFS, s)

            with pe.Fori(0, NH // GROUP - 1) as g:
                group(g, False)
            group(NH // GROUP - 1, True)


def output_projection(nc, x_t, wo_t, sum_scratch, rsum_scratch, xn_lo_scratch, xn_lo, acc):
    SUMS = NH * S // P
    with ExitStack() as ctx:
        def sb(name, shape, dt):
            return ctx.enter_context(nc.sbuf_tensor(name, shape, dt))

        def sem(name):
            return ctx.enter_context(nc.semaphore(name))

        sums = sb("sums", [P, SUMS], F32)
        rsums = sb("rsums", [P, SUMS], F32)
        wo_sb = sb("wo_sb", [P, KT, H], F32)
        rows = sb("rsum_rows", [P, NH // 4, S], F32)
        xt_sb = sb("xt_sb", [P, KT, S], F32)
        po = ctx.enter_context(nc.psum_tensor("po", [P, 2, KT, W], F32))
        loaded = sem("sums_loaded")
        wo_loaded = sem("wo_loaded")
        x_loaded = sem("xt_loaded")
        xn_lo_loaded = sem("xn_lo_loaded")
        inverted = sem("inverted")
        stored = sem("rsums_stored")
        rows_loaded = [sem(f"rows_loaded{g}") for g in range(NH // 4)]
        normalised = sem("normalised")
        projected = sem("o_projected")
        added = sem("o_added")
        block = ctx.enter_context(nc.Block())

        @block.sync
        def _(sp):
            sp.dma_start(sums[:, :], sum_scratch.rearrange("h (a b) -> (h a) b", b=SUMS)).then_inc(loaded, 16)
            sp.dma_start(wo_sb[:, :, :], wo_t.rearrange("(k p) o -> p k o", p=P)).then_inc(wo_loaded, 16)
            sp.dma_start(xt_sb[:, :, :], x_t.rearrange("(k p) t -> p k t", p=P)).then_inc(x_loaded, 16)
            sp.dma_start(xn_lo[:, :, :].bitcast(F32), xn_lo_scratch).then_inc(xn_lo_loaded, 16)
            sp.wait_ge(inverted, 1)
            sp.dma_start(rsum_scratch.rearrange("h (a b) -> (h a) b", b=SUMS), rsums[:, :]).then_inc(stored, 16)
            sp.wait_ge(stored, 16)
            for g in range(NH // 4):
                for j in range(4):
                    sp.dma_start(rows[j * D:(j + 1) * D, g, :],
                                 rsum_scratch[4 * g + j, :].partition_broadcast(D)).then_inc(rows_loaded[g], 16)
            sp.wait_ge(xn_lo_loaded, 16)

        @block.vector
        def _(dve):
            dve.wait_ge(loaded, 16)
            nc.vector.reciprocal(rsums[:, :], sums[:, :]).then_inc(inverted, 1)
            for g in range(NH // 4):
                dve.wait_ge(rows_loaded[g], 64)
                cols = slice(g * S, (g + 1) * S)
                nc.vector.tensor_tensor(acc[:, cols], acc[:, cols], rows[:, g, :],
                                        ALU.mult).then_inc(normalised, 1)
            dve.wait_ge(x_loaded, 16)
            for tc in range(TC):
                dve.wait_ge(projected, tc + 1)
                t = slice(tc * W, (tc + 1) * W)
                nc.vector.tensor_tensor(acc[:, :].rearrange("p (k t) -> p k t", k=KT)[:, :, t], xt_sb[:, :, t],
                                        po[:, tc % 2, :, :], ALU.add).then_inc(added, 1)

        @block.tensor
        def _(pe):
            pe.wait_ge(wo_loaded, 16)
            pe.wait_ge(normalised, NH // 4)
            for tc in range(TC):
                if tc >= 2:
                    pe.wait_ge(added, tc - 1)
                for ot in range(KT):
                    for g in range(NH // 4):
                        last = nc.tensor.matmul(po[:, tc % 2, ot, :], wo_sb[:, g, ot * P:(ot + 1) * P],
                                                acc[:, g * S + tc * W:g * S + (tc + 1) * W],
                                                start=g == 0, stop=g == NH // 4 - 1)
                last.then_inc(projected, 1)


def feed_forward(nc, gate_p, up_p, gate_up_s, down_p, down_s, xn_hi, xn_lo, acc, out_t):
    CN = 2 * P
    CHUNKS = MLP // CN
    PAIR = 2
    ROUND = PAIR * TC
    NB = 8
    REP = P // NB
    GELU_A = 0.044715
    GELU_B = 0.7978845608028654
    CODE_SCALE = float(2 ** 14)
    with ExitStack() as ctx:
        acc = acc[:, :].rearrange("p (k t) -> p k t", k=KT)

        def sb(name, shape, dt):
            return ctx.enter_context(nc.sbuf_tensor(name, shape, dt))

        def sem(name):
            return ctx.enter_context(nc.semaphore(name))

        packed = [sb(f"packed{i}", [P, 3, W], I32) for i in range(2)]
        scales = [sb(f"scales{i}", [P, 3, W], F32) for i in range(2)]
        high = sb("high", [P, W], I32)
        pair = sb("pair", [P, W], I32)
        magnitude = sb("magnitude", [P, W], I32)
        weight = sb("weight", [P, 2, W], F32)
        w_hi = [sb(f"w_hi{i}", [P, 3, 2, W], F32R) for i in range(2)]
        w_lo = [sb(f"w_lo{i}", [P, 3, 2, W], F32R) for i in range(2)]
        gate = sb("gate", [P, 2, W], F32)
        poly = sb("poly", [P, 2, W], F32)
        inter = sb("inter", [P, 2, W], F32)
        i_hi = sb("i_hi", [P, 2, 2, W], F32R)
        i_lo = sb("i_lo", [P, 2, 2, W], F32R)
        p_gate = ctx.enter_context(nc.psum_tensor("p_gate", [P, 2, W], F32))
        p_up = ctx.enter_context(nc.psum_tensor("p_up", [P, 2, W], F32))
        p_out = ctx.enter_context(nc.psum_tensor("p_out", [P, KT, W], F32))

        loaded = [sem(f"ffn_loaded{i}") for i in range(2)]
        unpacked = sem("unpacked")
        weight_hi = sem("weight_hi")
        weight_lo = sem("weight_lo")
        gate_done = sem("gate_done")
        up_done = sem("up_done")
        down_done = sem("down_done")
        gate_out = sem("gate_out")
        poly_done = sem("poly_done")
        pool_turns = sem("pool_turns")
        tanh_done = sem("tanh_done")
        gelu_done = sem("gelu_done")
        inter_done = sem("inter_done")
        i_hi_done = sem("i_hi_done")
        i_lo_done = sem("i_lo_done")
        added = sem("added")
        out_stored = sem("out_stored")
        block = ctx.enter_context(nc.Block())

        def load_chunk(sp, c, par):
            cols = bass.ds(c * CN, CN)
            for m, pk in enumerate((gate_p, up_p)):
                sp.dma_start(packed[par][:, m, :].rearrange("p (k n) -> p k n", k=2),
                             pk[:, cols].rearrange("(k p) n -> p k n", p=P)).then_inc(loaded[par], 16)
            sp.dma_start(packed[par][:, 2, :], down_p[bass.ds(c * P, P), :]).then_inc(loaded[par], 16)
            for b in range(NB):
                rows = slice(b * REP, (b + 1) * REP)
                sp.dma_start(scales[par][rows, 0:2, :].rearrange("p m (k n) -> p m k n", k=2),
                             gate_up_s[:, :, b, cols].partition_broadcast(REP)).then_inc(loaded[par], 16)
                sp.dma_start(scales[par][rows, 2, :], down_s[bass.ds(c * NB + b, 1), :].rearrange("a h -> (a h)")
                             .partition_broadcast(REP)).then_inc(loaded[par], 16)
        LOADED = 16 * (3 + 2 * NB)

        @block.sync
        def _(sp):
            load_chunk(sp, 0, 0)
            load_chunk(sp, 1, 1)

            def round_(i, last):
                for half in range(PAIR):
                    c = PAIR * i + half
                    if not last:
                        sp.wait_ge(weight_lo, 3 * (c + 1))
                        load_chunk(sp, c + 2, half)

            with sp.Fori(0, CHUNKS // PAIR - 1) as i:
                round_(i, False)
            for tc in range(TC):
                sp.wait_ge(added, (CHUNKS - 1) * TC + tc + 2)
                sp.dma_start(out_t[:, tc * W:(tc + 1) * W].rearrange("(k p) t -> p k t", p=P),
                             acc[:, :, tc * W:(tc + 1) * W]).then_inc(out_stored, 16)
            sp.wait_ge(out_stored, 16 * TC)

        def steps(eng, body):
            with eng.Fori(0, CHUNKS // PAIR - 1) as i:
                for j in range(ROUND):
                    body(i, j, False, j % TC == 3)
            for j in range(ROUND):
                body(CHUNKS // PAIR - 1, j, j == ROUND - 1, j % TC == 3 or j >= TC)

        def next_chunk(i, j):
            return PAIR * i + j // TC + 1, (j // TC + 1) % 2, i + 1 + j // TC

        @block.scalar
        def _(act):
            def hi_weights(c, par, m, first=False):
                act.wait_ge(unpacked, 7 * (3 * c + m + 1))
                if not first:
                    act.wait_ge(*((up_done, (c - 1) * TC + 1) if m < 2 else (down_done, (c - 1) * TC + 2)))
                nc.scalar.activation(w_hi[par][:, m, :, :], weight[:, :, :], ACT.Copy,
                                     scale=CODE_SCALE).then_inc(weight_hi, 1)

            def elementwise(n, buf):
                act.wait_ge(gate_done, n + 1)
                act.wait_ge(gelu_done, n + 1)
                nc.scalar.activation(gate[:, :, :], p_gate[:, :, :], ACT.Copy).then_inc(gate_out, 1)
                nc.scalar.activation(poly[:, :, :], p_gate[:, :, :], ACT.Square).then_inc(gate_out, 1)
                act.wait_ge(poly_done, 2 * n + 2)
                act.wait_ge(i_lo_done, n + 1)
                nc.scalar.activation(inter[:, :, :], poly[:, :, :], ACT.Tanh, scale=GELU_B).then_inc(tanh_done, 1)
                act.wait_ge(inter_done, n + 2)
                act.wait_ge(down_done, n + 1)
                nc.scalar.activation(i_hi[:, buf, :, :], inter[:, :, :], ACT.Copy).then_inc(i_hi_done, 1)

            def body(i, j, final, no_weights):
                if not no_weights:
                    c, par, _ = next_chunk(i, j)
                    hi_weights(c, par, j % TC)
                if not final:
                    elementwise(ROUND * i + j + 1, (j + 1) % 2)

            act.sem_inc(gate_out, 2)
            for m in range(3):
                hi_weights(0, 0, m, first=True)
            elementwise(0, 0)
            steps(act, body)

        @block.gpsimd
        def _(pool):
            def elementwise(n):
                pool.wait_ge(gate_out, 2 * n + 4)
                pool.sem_inc(pool_turns, 1)
                nc.gpsimd.tensor_scalar(poly[:, :, :], poly[:, :, :], GELU_A, 1.0, ALU.mult,
                                        ALU.add).then_inc(poly_done, 1)
                pool.wait_ge(poly_done, 2 * n + 1)
                nc.gpsimd.tensor_tensor(poly[:, :, :], poly[:, :, :], gate[:, :, :], ALU.mult).then_inc(poly_done, 1)

            def body(i, j, final, no_weights):
                if not final:
                    elementwise(ROUND * i + j + 1)

            elementwise(0)
            steps(pool, body)

        @block.vector
        def _(dve):
            def unpack(c, par, m, loads, first=False):
                k = 3 * c + m
                pk = packed[par][:, m, :]

                def own(step):
                    dve.wait_ge(unpacked, 7 * k + step)
                dve.wait_ge(loaded[par], LOADED * loads)
                if not (first and m == 0):
                    own(0)
                    dve.wait_ge(weight_lo, k)
                nc.vector.tensor_scalar(high[:, :], pk, 0xF0, 12, ALU.bitwise_and,
                                        ALU.logical_shift_left).then_inc(unpacked, 1)
                nc.vector.tensor_scalar(pair[:, :], pk, 0x0F, None, ALU.bitwise_and).then_inc(unpacked, 1)
                own(2)
                nc.vector.tensor_tensor(pair[:, :], pair[:, :], high[:, :], ALU.bitwise_or).then_inc(unpacked, 1)
                own(3)
                nc.vector.tensor_scalar(magnitude[:, :], pair[:, :], 0x00070007, 9, ALU.bitwise_and,
                                        ALU.logical_shift_left).then_inc(unpacked, 1)
                nc.vector.tensor_scalar(high[:, :], pair[:, :], 0x00080008, 12, ALU.bitwise_and,
                                        ALU.logical_shift_left).then_inc(unpacked, 1)
                own(5)
                nc.vector.tensor_tensor(magnitude[:, :], magnitude[:, :], high[:, :],
                                        ALU.bitwise_or).then_inc(unpacked, 1)
                own(6)
                codes = magnitude[:, :].bitcast(F16).rearrange("p (n a) -> p a n", a=2)
                sc = scales[par][:, m, :].unsqueeze(1).broadcast_to([P, 2, W])
                nc.vector.tensor_tensor(weight[:, :, :], codes, sc, ALU.mult).then_inc(unpacked, 1)

            def lo_weights(c, par, m):
                dve.wait_ge(weight_hi, 3 * c + m + 1)
                nc.vector.scalar_tensor_tensor(w_lo[par][:, m, :, :], weight[:, :, :], CODE_SCALE,
                                               w_hi[par][:, m, :, :].bitcast(F32), ALU.mult,
                                               ALU.subtract).then_inc(weight_lo, 1)

            def elementwise(n, buf):
                dve.wait_ge(tanh_done, n + 1)
                nc.vector.scalar_tensor_tensor(inter[:, :, :], inter[:, :, :], 1.0, gate[:, :, :],
                                               ALU.add, ALU.mult).then_inc(gelu_done, 1)
                dve.wait_ge(gelu_done, n + 2)
                dve.wait_ge(up_done, n + 2)
                nc.vector.scalar_tensor_tensor(inter[:, :, :], inter[:, :, :], 0.5, p_up[:, :, :],
                                               ALU.mult, ALU.mult).then_inc(inter_done, 1)
                dve.wait_ge(i_hi_done, n + 1)
                nc.vector.tensor_tensor(i_lo[:, buf, :, :], inter[:, :, :], i_hi[:, buf, :, :].bitcast(F32),
                                        ALU.subtract).then_inc(i_lo_done, 1)

            def body(i, j, final, no_weights):
                n = ROUND * i + j
                if not no_weights:
                    c, par, loads = next_chunk(i, j)
                    unpack(c, par, j % TC, loads)
                    lo_weights(c, par, j % TC)
                if not final:
                    elementwise(n + 1, (j + 1) % 2)
                dve.wait_ge(down_done, n + 3)
                here = acc[:, :, (j % TC) * W:(j % TC + 1) * W]
                nc.vector.tensor_tensor(here, here, p_out[:, :, :], ALU.add).then_inc(added, 1)

            dve.sem_inc(gelu_done, 1)
            dve.sem_inc(i_lo_done, 1)
            dve.sem_inc(inter_done, 1)
            dve.sem_inc(added, 1)
            for m in range(3):
                unpack(0, 0, m, 1, first=True)
                lo_weights(0, 0, m)
            elementwise(0, 0)
            steps(dve, body)

        @block.tensor
        def _(pe):
            def gate_and_up(i, j, n):
                par = j // TC % 2
                tokens = slice((j % TC) * W, (j % TC + 1) * W)
                for m, bank, free, done in ((0, p_gate, gate_out, gate_done), (1, p_up, inter_done, up_done)):
                    if j % TC == 0:
                        pe.wait_ge(weight_lo, 3 * (PAIR * i + j // TC) + m + 1)
                    pe.wait_ge(free, 2 * n + 2 if m == 0 else n + 1)
                    for nt in range(2):
                        for kt in range(KT):
                            rows = slice((kt % 2) * CN + nt * P, (kt % 2) * CN + (nt + 1) * P)
                            last = mm3(nc, bank[:, nt, :], w_hi[par][:, m, kt // 2, rows],
                                       w_lo[par][:, m, kt // 2, rows], xn_hi[:, kt, tokens], xn_lo[:, kt, tokens],
                                       kt == 0, kt == KT - 1)
                    last.then_inc(done, 1)

            def down(i, j, n):
                par = j // TC % 2
                if j % TC == 0:
                    pe.wait_ge(weight_lo, 3 * (PAIR * i + j // TC) + 3)
                pe.wait_ge(i_lo_done, n + 2)
                pe.wait_ge(added, n + 1)
                for ot in range(KT):
                    for nt in range(2):
                        last = mm3(nc, p_out[:, ot, :], w_hi[par][:, 2, nt, ot * P:(ot + 1) * P],
                                   w_lo[par][:, 2, nt, ot * P:(ot + 1) * P], i_hi[:, j % 2, nt, :],
                                   i_lo[:, j % 2, nt, :], nt == 0, nt == 1)
                last.then_inc(down_done, 1)

            def body(i, j, final, no_weights):
                n = ROUND * i + j
                if not final:
                    ni, nj = (i + 1, 0) if j == ROUND - 1 else (i, j + 1)
                    gate_and_up(ni, nj, n + 1)
                down(i, j, n)

            pe.sem_inc(up_done, 1)
            pe.sem_inc(down_done, 2)
            gate_and_up(0, 0, 0)
            steps(pe, body)


def layer(nc, x, x_t, wqkv_t, wo_t, gate_p, up_p, gate_up_s, down_p, down_s, out_t):
    qk_scratch = nc.dram_tensor("qk_scratch", (2, 2, H, S), F32).ap()
    v_scratch = nc.dram_tensor("v_scratch", (S, 2 * NH, D), F32).ap()
    sum_scratch = nc.dram_tensor("sum_scratch", (NH, S), F32).ap()
    rsum_scratch = nc.dram_tensor("rsum_scratch", (NH, S), F32).ap()
    xn_lo_scratch = nc.dram_tensor("xn_lo_scratch", (P, KT, S), F32).ap()
    with nc.sbuf_tensor("xn_hi", [P, KT, S], F32R) as xn_hi:
        with nc.sbuf_tensor("xn_lo_made", [P, KT, S], F32R) as xn_lo:
            norm_and_project(nc, x, wqkv_t, qk_scratch, v_scratch, xn_lo_scratch, xn_hi, xn_lo)
        with nc.sbuf_tensor("acc", [P, KT * S], F32) as acc:
            attention(nc, qk_scratch, v_scratch, sum_scratch, acc)
            with nc.sbuf_tensor("xn_lo", [P, KT, S], F32R) as xn_lo:
                output_projection(nc, x_t, wo_t, sum_scratch, rsum_scratch, xn_lo_scratch, xn_lo, acc)
                feed_forward(nc, gate_p, up_p, gate_up_s, down_p, down_s, xn_hi, xn_lo, acc, out_t)


def kernel(**inputs):
    import numpy as _np
    import concourse.bacc as _bacc
    from concourse import mybir as _mybir
    from concourse.bass_utils import run_bass_kernel_spmd as _run

    a = {k[3:]: _np.asarray(v) for k, v in inputs.items()}
    x = a["attn_hidden_states"].reshape(S, H)

    def by_tiles(w):
        return w.reshape(MLP // (2 * P), P, 2, -1).transpose(3, 0, 2, 1).reshape(w.shape[1], MLP)

    laid = {
        "x": x,
        "x_t": x.T,
        "wqkv_t": a["attn_w_qkv"].T.reshape(H // 2, 2, 3 * H).transpose(1, 0, 2).reshape(H, 3 * H),
        "wo_t": a["attn_w_o"].T,
        "gate_p": by_tiles(a["ffn_gate_W_packed"]),
        "up_p": by_tiles(a["ffn_up_W_packed"]),
        "gate_up_s": _np.stack([by_tiles(a["ffn_gate_scales"]), by_tiles(a["ffn_up_scales"])])
        .reshape(2, 2, H // 64, MLP),
        "down_p": a["ffn_down_W_packed"].T,
        "down_s": a["ffn_down_scales"].T,
    }
    nc = _bacc.Bacc("TRN2", target_bir_lowering=False, num_devices=1)
    arrays, args = {}, []
    for name, v in laid.items():
        v = _np.ascontiguousarray(v)
        arrays[f"in_{name}"] = v
        args.append(nc.dram_tensor(f"in_{name}", v.shape, _mybir.dt.from_np(v.dtype), kind="ExternalInput").ap())
    args.append(nc.dram_tensor("out_t", (H, S), _mybir.dt.float32, kind="ExternalOutput").ap())
    layer(nc, *args)
    r = _run(nc, [arrays], core_ids=[0])
    return _np.ascontiguousarray(r.results[0]["out_t"].T).reshape(1, S, H)
```

```python
import numpy as np
import concourse.bass as bass
from concourse import mybir
from contextlib import ExitStack

F32 = mybir.dt.float32
F32R = mybir.dt.float32r
BF16 = mybir.dt.bfloat16
F16 = mybir.dt.float16
I32 = mybir.dt.int32
ALU = mybir.AluOpType
ACT = mybir.ActivationFunctionType
AX = mybir.AxisListType

P = 128
S = 2048
H = 512
NH = 16
D = H // NH
MLP = 4096
KT = H // P
TT = S // P
W = 512
TC = S // W
EPS = 1e-5
MASKED = -float(2 ** 100)
NO_MAX = -3.0e38
SCALE = 1.0 / float(np.sqrt(np.float32(D)))


def mm3(nc, out, w_hi, w_lo, x_hi, x_lo, first, last):
    nc.tensor.matmul(out, w_hi, x_hi, start=first, stop=False)
    nc.tensor.matmul(out, w_hi, x_lo, start=False, stop=False)
    return nc.tensor.matmul(out, w_lo, x_hi, start=False, stop=last)


def norm_and_project(nc, x, wqkv_t, qk_scratch, v_scratch, xn_lo_scratch, xn_hi, xn_lo):
    LOADS = 4
    PER = TT // LOADS
    UNITS_QK = 2 * KT * TC
    UNITS = UNITS_QK + TT
    SLOTS = 4
    with ExitStack() as ctx:
        def sb(name, shape, dt):
            return ctx.enter_context(nc.sbuf_tensor(name, shape, dt))

        def sem(name):
            return ctx.enter_context(nc.semaphore(name))

        x_sb = sb("x_sb", [P, TT, H], F32)
        w_sb = sb("wqkv_sb", [P, KT, 3 * H], F32)
        w_hi = sb("wqkv_hi", [P, KT, 3 * H], F32R)
        w_lo = sb("wqkv_lo", [P, KT, 3 * H], F32R)
        ident = sb("ident1", [P, P], F32)
        stats = sb("stats", [P, TT, 6], F32)
        mean_var = sb("mean_var", [P, TT, 2], F32)
        var_eps = sb("var_eps", [P, TT], F32)
        std = sb("std", [P, TT], F32)
        rstd = sb("rstd", [P, TT], F32)
        out_hi = sb("out_hi", [P, SLOTS, W], F32R)
        out_lo = sb("out_lo", [P, SLOTS, W], F32R)
        out_v = sb("out_v", [P, 2, NH, 2, D], F32R)
        pt = ctx.enter_context(nc.psum_tensor("pt", [P, 2, W], F32))
        pj = ctx.enter_context(nc.psum_tensor("pj", [P, SLOTS, W], F32))

        x_loaded = [sem(f"x_loaded{i}") for i in range(LOADS)]
        w_loaded = [sem(f"w_loaded{i}") for i in range(3)]
        ident_made = sem("ident_made")
        stats_made = sem("stats_made")
        std_made = sem("std_made")
        rstd_made = sem("rstd_made")
        xn_made = sem("xn_made")
        transposed = sem("transposed")
        xn_hi_made = sem("xn_hi_made")
        xn_lo_made = sem("xn_lo_made")
        xn_lo_stored = sem("xn_lo_stored")
        w_hi_made = sem("w_hi_made")
        w_lo_made = sem("w_lo_made")
        projected = sem("projected")
        hi_made = sem("hi_made")
        lo_made = sem("lo_made")
        stored = [sem(f"stored{i}") for i in range(SLOTS)]
        stored_v = [sem(f"stored_v{i}") for i in range(2)]
        block = ctx.enter_context(nc.Block())

        @block.sync
        def _(sp):
            for i in range(LOADS):
                sp.dma_start(x_sb[:, i * PER:(i + 1) * PER, :],
                             x[i * PER * P:(i + 1) * PER * P, :].rearrange("(t p) h -> p t h", p=P)
                             ).then_inc(x_loaded[i], 16)
                if i < 3:
                    sp.dma_start(w_sb[:, :, i * H:(i + 1) * H],
                                 wqkv_t[:, i * H:(i + 1) * H].rearrange("(k p) o -> p k o", p=P)
                                 ).then_inc(w_loaded[i], 16)
            sp.wait_ge(xn_lo_made, TT)
            sp.dma_start(xn_lo_scratch, xn_lo[:, :, :].bitcast(F32)).then_inc(xn_lo_stored, 16)
            for u in range(UNITS):
                sp.wait_ge(hi_made, u + 1)
                sp.wait_ge(lo_made, u + 1)
                if u < UNITS_QK:
                    ot, tc = divmod(u, TC)
                    rows = slice((ot % KT) * P, (ot % KT + 1) * P)
                    for part, tile in ((0, out_hi), (1, out_lo)):
                        sp.dma_start(qk_scratch[ot // KT, part, rows, tc * W:(tc + 1) * W],
                                     tile[:, u % SLOTS, :].bitcast(F32)).then_inc(stored[u % SLOTS], 16)
                else:
                    tt = u - UNITS_QK
                    sp.dma_start(v_scratch[tt * P:(tt + 1) * P, :, :],
                                 out_v[:, tt % 2, :, :, :].rearrange("p h a d -> p h (a d)").bitcast(F32)
                                 ).then_inc(stored_v[tt % 2], 16)
            sp.wait_ge(xn_lo_stored, 16)
            for s in range(SLOTS):
                sp.wait_ge(stored[s], 32 * (UNITS_QK // SLOTS))
            for s in range(2):
                sp.wait_ge(stored_v[s], 16 * (TT // 2))

        @block.gpsimd
        def _(pool):
            nc.gpsimd.memset(ident[:, :], 0.0).then_inc(ident_made, 1)
            pool.wait_ge(ident_made, 1)
            nc.gpsimd.affine_select(out=ident[:, :], in_=ident[:, :], compare_op=ALU.not_equal, fill=1.0,
                                    base=0, pattern=[[-1, P]], channel_multiplier=1).then_inc(ident_made, 1)

        @block.scalar
        def _(act):
            def root(i):
                act.wait_ge(stats_made, (2 * PER + 1) * (i + 1))
                cols = slice(i * PER, (i + 1) * PER)
                nc.scalar.activation(std[:, cols], var_eps[:, cols], ACT.Sqrt).then_inc(std_made, 1)

            root(0)
            for i in range(LOADS):
                if i + 1 < LOADS:
                    root(i + 1)
                if i > 0:
                    act.wait_ge(w_loaded[i - 1], 16)
                    nc.scalar.activation(w_hi[:, :, (i - 1) * H:i * H], w_sb[:, :, (i - 1) * H:i * H],
                                         ACT.Copy).then_inc(w_hi_made, 1)
                for tt in range(i * PER, (i + 1) * PER):
                    act.wait_ge(transposed, tt + 1)
                    nc.scalar.activation(xn_hi[:, :, tt * P:(tt + 1) * P],
                                         pt[:, tt % 2, :].rearrange("p (k t) -> p k t", k=KT),
                                         ACT.Copy).then_inc(xn_hi_made, 1)
            for u in range(UNITS):
                act.wait_ge(projected, u + 1)
                if u < UNITS_QK:
                    if u >= SLOTS:
                        act.wait_ge(stored[u % SLOTS], 32 * (u // SLOTS))
                    nc.scalar.activation(out_hi[:, u % SLOTS, :], pj[:, u % SLOTS, :],
                                         ACT.Copy).then_inc(hi_made, 1)
                else:
                    tt = u - UNITS_QK
                    if tt >= 2:
                        act.wait_ge(stored_v[tt % 2], 16 * (tt // 2))
                    nc.scalar.activation(out_v[:, tt % 2, :, 0, :],
                                         pj[:, u % SLOTS, :].rearrange("p (h d) -> p h d", h=NH),
                                         ACT.Copy).then_inc(hi_made, 1)

        @block.vector
        def _(dve):
            def norm(i):
                n = (2 * PER + 1) * i
                cols = slice(i * PER, (i + 1) * PER)
                dve.wait_ge(x_loaded[i], 16)
                for tt in range(i * PER, (i + 1) * PER):
                    nc.vector.bn_stats(stats[:, tt, :], x_sb[:, tt, :]).then_inc(stats_made, 1)
                for k, tt in enumerate(range(i * PER, (i + 1) * PER)):
                    dve.wait_ge(stats_made, n + PER + k)
                    nc.vector.bn_aggr(mean_var[:, tt, :], stats[:, tt, :]).then_inc(stats_made, 1)
                dve.wait_ge(stats_made, n + 2 * PER)
                nc.vector.tensor_scalar(var_eps[:, cols], mean_var[:, cols, 1], EPS, None,
                                        ALU.add).then_inc(stats_made, 1)
                dve.wait_ge(std_made, i + 1)
                nc.vector.reciprocal(rstd[:, cols], std[:, cols]).then_inc(rstd_made, 1)
                dve.wait_ge(rstd_made, i + 1)
                for tt in range(i * PER, (i + 1) * PER):
                    nc.vector.tensor_scalar(x_sb[:, tt, :], x_sb[:, tt, :], mean_var[:, tt, 0:1],
                                            rstd[:, tt:tt + 1], ALU.subtract, ALU.mult).then_inc(xn_made, 1)

            norm(0)
            for i in range(LOADS):
                if i + 1 < LOADS:
                    norm(i + 1)
                if i > 0:
                    dve.wait_ge(w_hi_made, i)
                    cols = slice((i - 1) * H, i * H)
                    nc.vector.tensor_tensor(w_lo[:, :, cols], w_sb[:, :, cols], w_hi[:, :, cols].bitcast(F32),
                                            ALU.subtract).then_inc(w_lo_made, 1)
                for tt in range(i * PER, (i + 1) * PER):
                    dve.wait_ge(xn_hi_made, tt + 1)
                    cols = slice(tt * P, (tt + 1) * P)
                    nc.vector.tensor_tensor(xn_lo[:, :, cols],
                                            pt[:, tt % 2, :].rearrange("p (k t) -> p k t", k=KT),
                                            xn_hi[:, :, cols].bitcast(F32), ALU.subtract).then_inc(xn_lo_made, 1)
            for u in range(UNITS):
                dve.wait_ge(hi_made, u + 1)
                if u < UNITS_QK:
                    nc.vector.tensor_tensor(out_lo[:, u % SLOTS, :], pj[:, u % SLOTS, :],
                                            out_hi[:, u % SLOTS, :].bitcast(F32), ALU.subtract).then_inc(lo_made, 1)
                else:
                    tt = u - UNITS_QK
                    nc.vector.tensor_tensor(out_v[:, tt % 2, :, 1, :],
                                            pj[:, u % SLOTS, :].rearrange("p (h d) -> p h d", h=NH),
                                            out_v[:, tt % 2, :, 0, :].bitcast(F32), ALU.subtract).then_inc(lo_made, 1)

        @block.tensor
        def _(pe):
            pe.wait_ge(ident_made, 2)
            for tt in range(TT):
                pe.wait_ge(xn_made, tt + 1)
                if tt >= 2:
                    pe.wait_ge(xn_lo_made, tt - 1)
                for kt in range(KT):
                    par, half = divmod(kt, 2)
                    first = 2 * P * half + par
                    last = nc.tensor.transpose(pt[:, tt % 2, kt * P:(kt + 1) * P],
                                               x_sb[:, tt, first:first + 2 * P - 1:2], ident[:, :])
                last.then_inc(transposed, 1)
            pe.wait_ge(xn_lo_made, TT)
            for u in range(UNITS):
                if u % (KT * TC) == 0:
                    pe.wait_ge(w_lo_made, u // (KT * TC) + 1)
                if u >= SLOTS:
                    pe.wait_ge(lo_made, u - SLOTS + 1)
                for kt in range(KT):
                    if u < UNITS_QK:
                        ot, tc = divmod(u, TC)
                        o, t = slice(ot * P, (ot + 1) * P), slice(tc * W, (tc + 1) * W)
                        last = mm3(nc, pj[:, u % SLOTS, :], w_hi[:, kt, o], w_lo[:, kt, o],
                                   xn_hi[:, kt, t], xn_lo[:, kt, t], kt == 0, kt == KT - 1)
                    else:
                        tt = u - UNITS_QK
                        o, t = slice(2 * H, 3 * H), slice(tt * P, (tt + 1) * P)
                        last = mm3(nc, pj[:, u % SLOTS, :], xn_hi[:, kt, t], xn_lo[:, kt, t],
                                   w_hi[:, kt, o], w_lo[:, kt, o], kt == 0, kt == KT - 1)
                last.then_inc(projected, 1)


def attention(nc, qk_scratch, v_scratch, sum_scratch, rsum_scratch, wo_t, wo_sb, attn_t):
    GROUP = 4
    ROWS = 3 * D
    VW = 3 * D
    CAP = W
    QK_BUFS = GROUP
    V_BUFS = 2
    E_BUFS = 4
    LEAD, HI_LEAD, LO_LEAD = 3, 2, 1
    UNITS = [(i, k, min(CAP, P * (i + 1) - k)) for i in range(TT) for k in range(0, P * (i + 1), CAP)]
    NU = len(UNITS)
    STEPS = [(qc, pair, 0 if pair < 2 * qc + 1 else W // 2) for qc in range(TC) for pair in range(2 * qc + 2)]
    NS = len(STEPS)
    WHOLE = {8, 13, 17}
    POOL_HI = set(range(NS))
    POOL_LO = {3, 6, 11, 16}
    LAST = [s for s in range(NS) if s + 1 == NS or STEPS[s + 1][0] != STEPS[s][0]]
    CHAIN = 3 * NS // 4
    BESIDE = {s: [] for s in range(NS)}
    for u in range(NU):
        ahead, s = divmod(CHAIN + u * NS // NU, NS)
        BESIDE[s].append((2 - ahead, u))
    HI = [None if s in WHOLE else "pool" if s in POOL_HI else "act" for s in range(NS)]
    LO = [None if s in WHOLE else "pool" if s in POOL_LO else "dve" for s in range(NS)]
    NORMALISE = {(j, s): [] for j in range(GROUP) for s in range(NS)}
    for n in range(2 * TC):
        NORMALISE[GROUP - 2, CHAIN + 1 + n // 2].append((n // TC, n % TC, False))
    for n in range(2 * TC):
        NORMALISE[GROUP - 1, n + 6].append((2 + n // TC, n % TC, False))
    for qc in range(TC - 1):
        NORMALISE[GROUP - 1, LAST[qc] + 4].append((NH // GROUP - 1, qc, True))
    CREDIT = 4

    def made(parts, who, h, s):
        whole, part = divmod(s, NS)
        return (h + whole) * parts.count(who) + parts[:part + 1].count(who) + CREDIT

    with ExitStack() as ctx:
        def sb(name, shape, dt):
            return ctx.enter_context(nc.sbuf_tensor(name, shape, dt))

        def sem(name):
            return ctx.enter_context(nc.semaphore(name))

        q_stack = [sb(f"q_stack{i}", [P, S], F32R) for i in range(QK_BUFS)]
        k_stack = [sb(f"k_stack{i}", [P, S], F32R) for i in range(QK_BUFS)]
        v_stack = [sb(f"v_stack{i}", [P, TT, VW], F32R) for i in range(V_BUFS)]
        e_sb = sb("e_sb", [P, E_BUFS, 2, W], F32)
        e_hi = sb("e_hi", [P, E_BUFS, 2, W], F32R)
        e_lo = sb("e_lo", [P, E_BUFS, 2, W], F32R)
        lo_sum = sb("lo_sum", [D + 1, 2, W], F32)
        recip = sb("recip", [P, W], F32)
        COMPACT = 3 * D
        compact, rcompact = recip[0:COMPACT, 0:W // 2], recip[0:COMPACT, W // 2:]
        max_part = sb("max_part", [P, TT, TC], F32)
        row_max = sb("row_max", [P, TT], F32)
        rest1 = sb("rest1", [P, TT], F32)
        rest2 = sb("rest2", [P, TT], F32)
        max_cols = sb("max_cols", [P, TT, P], BF16)
        ident = sb("ident_bf", [P, P], BF16)
        mask_q = sb("mask_q", [P, P], BF16)
        mask_k = sb("mask_k", [P, 2 * P], BF16)
        p_st = ctx.enter_context(nc.psum_tensor("p_st", [P, 2, 2, W], F32))
        p_s = ctx.enter_context(nc.psum_tensor("p_s", [P, 2, W], F32))
        p_o = ctx.enter_context(nc.psum_tensor("p_o", [P, 2, W], F32))

        consts = sem("consts")
        minus_one = sem("minus_one")
        pool_turns = sem("pool_turns_attn")
        qk_loaded = [sem(f"qk_loaded{i}") for i in range(QK_BUFS)]
        v_loaded = [sem(f"v_loaded{i}") for i in range(V_BUFS)]
        scored = sem("scored")
        maxed = sem("maxed")
        max_step = sem("max_step")
        max_split = sem("max_split")
        max_turned = sem("max_turned")
        max_rows = sem("max_rows")
        st_ready = sem("st_ready")
        exp_done = sem("exp_done")
        hi_made = {who: sem(f"e_hi_made_{who}") for who in ("act", "pool")}
        lo_made = {who: sem(f"e_lo_made_{who}") for who in ("dve", "pool")}
        pv_done = sem("pv_done")
        lo_sum_made = sem("lo_sum_made")
        o_free = sem("o_free")
        rows_loaded = [sem(f"rows_loaded{g}") for g in range(NH // GROUP)]
        last_rows = [sem(f"last_rows{qc}") for qc in range(TC)]
        sums_loaded = sem("sums_loaded")
        sums_inverted = sem("sums_inverted")
        rsums_out = sem("rsums_out")
        inverted = sem("inverted")
        normalised = sem("normalised")
        wo_loaded = sem("wo_loaded")
        sums_out = [sem(f"sums_out{i}") for i in range(2)]
        block = ctx.enter_context(nc.Block())
        NC = 6

        def load_qk(sp, h, par):
            rows = bass.ds(h * D, D)
            for strip, part in enumerate((0, 0, 1)):
                sp.dma_start(q_stack[par][strip * D:(strip + 1) * D, :].bitcast(F32),
                             qk_scratch[0, part, rows, :]).then_inc(qk_loaded[par], 16)
            for strip, part in enumerate((0, 1, 0)):
                sp.dma_start(k_stack[par][strip * D:(strip + 1) * D, :].bitcast(F32),
                             qk_scratch[1, part, rows, :]).then_inc(qk_loaded[par], 16)

        sum_rows = [t[:, :].bitcast(F32) for t in (q_stack[0], k_stack[0], q_stack[1], k_stack[1])]

        def load_row(sp, scratch, h, loaded, cols=slice(0, S)):
            sp.dma_start(sum_rows[h // GROUP][h % GROUP * D:(h % GROUP + 1) * D, cols],
                         scratch[h, cols].partition_broadcast(D)).then_inc(loaded, 16)

        def load_v(sp, h, par):
            for part, col in ((0, 2 * D), (1, 0)):
                sp.dma_start(v_stack[par][:, :, col:col + D].bitcast(F32),
                             v_scratch[:, bass.ds(2 * h + part, 1), :].rearrange("(t p) a d -> p t (a d)", p=P)
                             ).then_inc(v_loaded[par], 16)

        @block.sync
        def _(sp):
            load_qk(sp, 0, 0)
            load_v(sp, 0, 0)
            for h in range(1, QK_BUFS - 1):
                load_qk(sp, h, h)
            sp.dma_start(wo_sb[:, :, :], wo_t.rearrange("(k p) o -> p k o", p=P)).then_inc(wo_loaded, 16)

            def invert_sums(h, heads):
                n = 1 if h else 0
                for sums in sums_out:
                    sp.wait_ge(sums, 16 * (TC // 2 * (h + heads) + 1))
                sp.dma_start(compact[:, 0:heads * S // COMPACT],
                             sum_scratch[h:h + heads, :].rearrange("h (a b) -> (h a) b", b=heads * S // COMPACT)
                             ).then_inc(sums_loaded, 16)
                sp.wait_ge(sums_inverted, n + 1)
                sp.dma_start(rsum_scratch[h:h + heads, :].rearrange("h (a b) -> (h a) b", b=heads * S // COMPACT),
                             rcompact[:, 0:heads * S // COMPACT]).then_inc(rsums_out, 16)
                sp.wait_ge(rsums_out, 16 * (n + 1))

            def rows_for_normalisation(j):
                if j == 1:
                    invert_sums(0, 3 * GROUP)
                    for h in range(2 * GROUP):
                        load_row(sp, rsum_scratch, h, rows_loaded[h // GROUP])
                elif j == 2:
                    for h in range(2 * GROUP, 3 * GROUP):
                        load_row(sp, rsum_scratch, h, rows_loaded[2])
                else:
                    invert_sums(3 * GROUP, GROUP - 1)
                    for h in range(3 * GROUP, NH - 1):
                        load_row(sp, rsum_scratch, h, rows_loaded[3])

            def group(g, last):
                for j in range(GROUP):
                    h = g * GROUP + j
                    sp.wait_ge(pv_done, h * NS + E_BUFS)
                    if not (last and j + 1 >= GROUP):
                        load_v(sp, h + 1, (j + 1) % V_BUFS)
                    if not (last and j + QK_BUFS - 1 >= GROUP):
                        load_qk(sp, h + QK_BUFS - 1, (j + QK_BUFS - 1) % QK_BUFS)
                    for qc in range(TC):
                        sp.wait_ge(lo_sum_made, h * TC + qc + 1)
                        sp.dma_start(sum_scratch[bass.ds(h, 1), qc * W:(qc + 1) * W],
                                     lo_sum[D:D + 1, qc % 2, :]).then_inc(sums_out[qc % 2], 16)
                        if last and qc == 0 and j > 0:
                            rows_for_normalisation(j)
                        if last and j == GROUP - 1:
                            sp.wait_ge(sums_out[qc % 2], 16 * (h * (TC // 2) + qc // 2 + 2))
                            load_row(sp, sum_scratch, h, last_rows[qc], slice(qc * W, (qc + 1) * W))

            sp.sem_inc(sums_out[0], 16)
            sp.sem_inc(sums_out[1], 16)
            with sp.Fori(0, NH // GROUP - 1) as g:
                group(g, False)
            group(NH // GROUP - 1, True)
            sp.wait_ge(wo_loaded, 16)

        def ahead(g, j, s, steps, last):
            dj, s = divmod(s + steps, NS)
            if last and j + dj >= GROUP:
                return None
            return g * GROUP + j + dj, (j + dj) % GROUP, s

        def make_hi(eng, h, s):
            who, n, w = HI[s], h * NS + s, W - STEPS[s][2]
            eng.wait_ge(exp_done, n + 3)
            eng.wait_ge(pv_done, n + 1)
            if who == "act":
                nc.scalar.activation(e_hi[:, s % E_BUFS, :, 0:w], e_sb[:, s % E_BUFS, :, 0:w],
                                     ACT.Copy).then_inc(hi_made["act"], 1)
            else:
                eng.sem_inc(pool_turns, 1)
                nc.gpsimd.tensor_scalar(e_hi[:, s % E_BUFS, :, 0:w], e_sb[:, s % E_BUFS, :, 0:w], 1.0, 1.0, ALU.mult,
                                        ALU.mult).then_inc(hi_made["pool"], 1)

        def make_lo(eng, h, s):
            who, w = LO[s], W - STEPS[s][2]
            eng.wait_ge(hi_made[HI[s]], made(HI, HI[s], h, s))
            eng.wait_ge(pv_done, h * NS + s + 1)
            engine = nc.gpsimd if who == "pool" else nc.vector
            engine.tensor_tensor(e_lo[:, s % E_BUFS, :, 0:w], e_sb[:, s % E_BUFS, :, 0:w],
                                 e_hi[:, s % E_BUFS, :, 0:w].bitcast(F32), ALU.subtract).then_inc(lo_made[who], 1)

        @block.gpsimd
        def _(pool):
            nc.gpsimd.memset(ident[:, :], 0.0).then_inc(consts, 1)
            nc.gpsimd.memset(mask_q[:, :], 0.0).then_inc(consts, 1)
            nc.gpsimd.memset(mask_k[:, 0:P], MASKED).then_inc(consts, 1)
            nc.gpsimd.memset(mask_k[:, P:], 0.0).then_inc(consts, 1)
            nc.gpsimd.memset(max_cols[:, :, :], 0.0).then_inc(consts, 1)
            nc.gpsimd.memset(max_part[:, :, :], NO_MAX).then_inc(consts, 1)
            pool.wait_ge(consts, NC)
            nc.gpsimd.affine_select(out=ident[:, :], in_=ident[:, :], compare_op=ALU.not_equal, fill=1.0,
                                    base=0, pattern=[[-1, P]], channel_multiplier=1).then_inc(consts, 1)
            nc.gpsimd.affine_select(out=mask_q[:, :], in_=mask_q[:, :], compare_op=ALU.is_ge, fill=MASKED,
                                    base=0, pattern=[[-1, P]], channel_multiplier=1).then_inc(consts, 1)
            nc.gpsimd.affine_select(out=mask_k[:, P:], in_=mask_k[:, P:], compare_op=ALU.is_ge, fill=MASKED,
                                    base=0, pattern=[[1, P]], channel_multiplier=-1).then_inc(consts, 1)
            pool.wait_ge(consts, NC + 3)
            for n, k in enumerate(k_stack):
                nc.gpsimd.memset(k[ROWS:P, :].bitcast(F32), 0.0).then_inc(minus_one, 1)
                pool.wait_ge(minus_one, 2 * n + 1)
                nc.gpsimd.memset(k[ROWS:ROWS + 3, :].bitcast(F32), -1.0).then_inc(minus_one, 1)
                pool.wait_ge(minus_one, 2 * n + 2)
            for n, v in enumerate(v_stack, QK_BUFS):
                nc.gpsimd.memset(v[:, :, D:2 * D].bitcast(F32), 0.0).then_inc(minus_one, 1)
                pool.wait_ge(minus_one, 2 * n + 1)
                nc.gpsimd.memset(v[:, :, D:D + 1].bitcast(F32), 1.0).then_inc(minus_one, 1)
                pool.wait_ge(minus_one, 2 * n + 2)
            pool.sem_inc(hi_made["pool"], CREDIT)
            pool.sem_inc(lo_made["pool"], CREDIT)

            def hi(h, s):
                if HI[s] == "pool":
                    make_hi(pool, h, s)

            def lo(h, s):
                if LO[s] == "pool":
                    make_lo(pool, h, s)

            def group(g, last):
                for j in range(GROUP):
                    for s in range(NS):
                        if (at := ahead(g, j, s, HI_LEAD, last)) is not None:
                            hi(at[0], at[2])
                        if (at := ahead(g, j, s, LO_LEAD, last)) is not None:
                            lo(at[0], at[2])

            for s in range(HI_LEAD):
                hi(0, s)
            for s in range(LO_LEAD):
                lo(0, s)
            with pool.Fori(0, NH // GROUP - 1) as g:
                group(g, False)
            group(NH // GROUP - 1, True)

        @block.scalar
        def _(act):
            def max_row(h, par, r):
                act.wait_ge(max_turned, h * TC + r + 1)
                nc.scalar.activation(q_stack[par][ROWS:P, r * W:(r + 1) * W], p_o[ROWS:P, 0, :],
                                     ACT.Copy).then_inc(max_rows, 1)

            def exps(h, s):
                qc, pair, q0 = STEPS[s]
                w = W - q0
                act.wait_ge(st_ready, h * NS + s + 1)
                before = s - E_BUFS
                if before % NS in WHOLE:
                    act.wait_ge(pv_done, h * NS + s + 1)
                else:
                    act.wait_ge(lo_made[LO[before]], made(LO, LO[before], h, before))
                nc.scalar.activation(e_sb[:, s % E_BUFS, :, 0:w], p_st[:, s % 2, :, 0:w], ACT.Exp,
                                     scale=SCALE).then_inc(exp_done, 1)

            def lower_part(h, s):
                qc = STEPS[s][0]
                act.wait_ge(pv_done, h * NS + s + 1 + E_BUFS)
                act.wait_ge(sums_out[qc % 2], (h * 2 + qc // 2 + 1) * 16)
                nc.scalar.activation(lo_sum[:, qc % 2, :], p_o[0:D + 1, qc % 2, :],
                                     ACT.Copy).then_inc(lo_sum_made, 1)

            act.sem_inc(exp_done, 2)
            act.sem_inc(hi_made["act"], CREDIT)
            for r in range(TC):
                max_row(0, 0, r)
            for s in range(LEAD):
                exps(0, s)
                if s < LEAD - 1 and HI[s] == "act":
                    make_hi(act, 0, s)

            def group(g, last):
                for j in range(GROUP):
                    h = g * GROUP + j
                    final = last and j == GROUP - 1
                    for s in range(NS):
                        if (at := ahead(g, j, s, LEAD - 1, last)) is not None and HI[at[2]] == "act":
                            make_hi(act, at[0], at[2])
                        if (at := ahead(g, j, s, LEAD, last)) is not None:
                            exps(at[0], at[2])
                        if s >= NS - TC and not final:
                            max_row(h + 1, (j + 1) % QK_BUFS, s - (NS - TC))
                        if s - 1 in LAST:
                            lower_part(h, s - 1)
                    lower_part(h, NS - 1)

            with act.Fori(0, NH // GROUP - 1) as g:
                group(g, False)
            group(NH // GROUP - 1, True)

        @block.vector
        def _(dve):
            dve.wait_ge(consts, NC)
            dve.sem_inc(lo_made["dve"], CREDIT)
            dve.sem_inc(o_free, 2)

            def unit_max(h, u):
                i, k, w = UNITS[u]
                dve.wait_ge(scored, h * NU + u + 1)
                nc.vector.reduce_max(max_part[:, i, k // CAP:k // CAP + 1],
                                     p_s[:, u % 2, 0:w], AX.X).then_inc(maxed, 1)

            def split_max(h, first=False):
                dve.wait_ge(maxed, (h + 1) * NU + 2)
                if not first:
                    dve.wait_ge(max_turned, h * TC)
                nc.vector.reduce_max(row_max[:, :], max_part[:, :, :], AX.X).then_inc(max_step, 1)
                dve.wait_ge(max_step, h * 5 + 1)
                nc.vector.tensor_copy(max_cols[:, :, ROWS], row_max[:, :]).then_inc(max_step, 1)
                dve.wait_ge(max_step, h * 5 + 2)
                nc.vector.tensor_tensor(rest1[:, :], row_max[:, :], max_cols[:, :, ROWS],
                                        ALU.subtract).then_inc(max_step, 1)
                dve.wait_ge(max_step, h * 5 + 3)
                nc.vector.tensor_copy(max_cols[:, :, ROWS + 1], rest1[:, :]).then_inc(max_step, 1)
                dve.wait_ge(max_step, h * 5 + 4)
                nc.vector.tensor_tensor(rest2[:, :], rest1[:, :], max_cols[:, :, ROWS + 1],
                                        ALU.subtract).then_inc(max_step, 1)
                dve.wait_ge(max_step, h * 5 + 5)
                nc.vector.tensor_copy(max_cols[:, :, ROWS + 2], rest2[:, :]).then_inc(max_split, 1)

            def add_parts(g, h, j, qc):
                dve.wait_ge(lo_sum_made, h * TC + qc + 1)
                nc.vector.tensor_tensor(attn_t[j * D:(j + 1) * D, bass.ds(g * S + qc * W, W)],
                                        p_o[2 * D:VW, qc % 2, :], lo_sum[0:D, qc % 2, :],
                                        ALU.add).then_inc(o_free, 1)

            for u in range(NU):
                unit_max(0, u)
            split_max(0, first=True)
            for s in range(CHAIN, NS):
                for heads, u in BESIDE[s]:
                    unit_max(heads - 1, u)
            for s in range(LO_LEAD):
                if LO[s] == "dve":
                    make_lo(dve, 0, s)

            def invert_compact(n, heads):
                dve.wait_ge(sums_loaded, 16 * (n + 1))
                if n:
                    dve.wait_ge(rsums_out, 16 * n)
                cols = slice(0, heads * S // COMPACT)
                nc.vector.reciprocal(rcompact[:, cols], compact[:, cols]).then_inc(sums_inverted, 1)

            def normalise(g, qc, last_head):
                cols = slice(qc * W, (qc + 1) * W)
                heads = slice(0, P) if g < NH // GROUP - 1 else slice(P - D, P) if last_head else slice(0, P - D)
                factor = sum_rows[g][heads, cols]
                if last_head:
                    dve.wait_ge(last_rows[qc], 16)
                    if qc:
                        dve.wait_ge(normalised, qc)
                    nc.vector.reciprocal(recip[heads, :], factor).then_inc(inverted, 1)
                    factor = recip[heads, :]
                    dve.wait_ge(inverted, qc + 1)
                    dve.wait_ge(o_free, (NH - 1) * TC + qc + 3)
                else:
                    dve.wait_ge(rows_loaded[g], 16 * min(GROUP, NH - 1 - g * GROUP))
                chunk = attn_t[heads, g * S + qc * W:g * S + (qc + 1) * W]
                last = nc.vector.tensor_tensor(chunk, chunk, factor, ALU.mult)
                if last_head:
                    last.then_inc(normalised, 1)

            def group(g, last):
                for j in range(GROUP):
                    h = g * GROUP + j
                    for s in range(NS):
                        if last and (j, s) in ((1, 4), (GROUP - 1, 4)):
                            invert_compact(j // 2, 3 * GROUP if j == 1 else GROUP - 1)
                        if last:
                            for piece in NORMALISE[j, s]:
                                normalise(*piece)
                        if s == CHAIN and not (last and j + 1 >= GROUP):
                            split_max(h + 1)
                        if (at := ahead(g, j, s, LO_LEAD, last)) is not None and LO[at[2]] == "dve":
                            make_lo(dve, at[0], at[2])
                        for heads, u in BESIDE[s]:
                            if not (last and j + heads >= GROUP):
                                unit_max(h + heads, u)
                        if s - 1 in LAST:
                            add_parts(g, h, j, STEPS[s - 1][0])
                    add_parts(g, h, j, TC - 1)
                if last:
                    normalise(g, TC - 1, True)

            with dve.Fori(0, NH // GROUP - 1) as g:
                group(g, False)
            group(NH // GROUP - 1, True)

        @block.tensor
        def _(pe):
            pe.sem_inc(pv_done, E_BUFS)
            pe.wait_ge(consts, NC + 3)

            def scores(h, par, u):
                i, k, w = UNITS[u]
                diagonal = k + w == P * (i + 1)
                pe.wait_ge(maxed, h * NU + u + 1)
                last = nc.tensor.matmul(p_s[:, u % 2, 0:w], q_stack[par][0:ROWS, i * P:(i + 1) * P],
                                        k_stack[par][0:ROWS, k:k + w], start=True, stop=not diagonal)
                if diagonal:
                    last = nc.tensor.matmul(p_s[:, u % 2, w - P:w], ident[:, :], mask_q[:, :],
                                            start=False, stop=True)
                last.then_inc(scored, 1)

            def turn_max(h, r):
                if r == 0:
                    pe.wait_ge(max_split, h + 1)
                    pe.wait_ge(o_free, h * TC + 1)
                pe.wait_ge(max_rows, h * TC + r + 1)
                for t in range(W // P):
                    last = nc.tensor.matmul(p_o[:, 0, t * P:(t + 1) * P], max_cols[:, r * (W // P) + t, :],
                                            ident[:, :], start=True, stop=True)
                last.then_inc(max_turned, 1)

            def scores_t(h, par, s):
                qc, pair, q0 = STEPS[s]
                w = W - q0
                if pair == 0:
                    pe.wait_ge(max_rows, h * TC + qc + 2)
                pe.wait_ge(exp_done, h * NS + s + 1)
                for t in range(2):
                    kt = 2 * pair + t
                    diagonal = kt * P >= qc * W
                    last = nc.tensor.matmul(p_st[:, s % 2, t, 0:w], k_stack[par][:, kt * P:(kt + 1) * P],
                                            q_stack[par][:, qc * W + q0:(qc + 1) * W], start=True,
                                            stop=not diagonal)
                    if diagonal:
                        last = nc.tensor.matmul(p_st[:, s % 2, t, 0:(t + 1) * P], ident[:, :],
                                                mask_k[:, (1 - t) * P:], start=False, stop=True)
                last.then_inc(st_ready, 1)

            def product_v(h, par, s):
                qc, pair, q0 = STEPS[s]
                w = W - q0
                if pair == 0:
                    pe.wait_ge(o_free, h * TC + qc + 1)
                if s == 0:
                    pe.wait_ge(max_rows, (h + 1) * TC + 1)
                final_step = s in LAST
                if s in WHOLE:
                    pe.wait_ge(exp_done, h * NS + s + 3)
                    for t in range(2):
                        last = nc.tensor.matmul(p_o[0:VW, qc % 2, q0:], v_stack[par][:, 2 * pair + t, :].bitcast(F32),
                                                e_sb[:, s % E_BUFS, t, 0:w], start=(pair == 0 and t == 0),
                                                stop=(final_step and t == 1))
                    last.then_inc(pv_done, 1)
                    return
                pe.wait_ge(hi_made[HI[s]], made(HI, HI[s], h, s))
                for part, tile in ((0, e_hi), (1, e_lo)):
                    if part:
                        pe.wait_ge(lo_made[LO[s]], made(LO, LO[s], h, s))
                    for t in range(2):
                        last = nc.tensor.matmul(p_o[0:VW, qc % 2, q0:], v_stack[par][:, 2 * pair + t, :],
                                                tile[:, s % E_BUFS, t, 0:w], start=(pair == 0 and part == 0 and t == 0),
                                                stop=(final_step and part == 1 and t == 1))
                last.then_inc(pv_done, 1)

            pe.sem_inc(maxed, 2)
            pe.sem_inc(max_rows, 1)
            for u in range(NU):
                if u == 0:
                    pe.wait_ge(qk_loaded[0], 96)
                scores(0, 0, u)
            for r in range(TC):
                turn_max(0, r)
            pe.wait_ge(minus_one, 2 * (QK_BUFS + V_BUFS))
            for s in range(LEAD):
                scores_t(0, 0, s)
            for s in range(CHAIN, NS):
                for heads, u in BESIDE[s]:
                    if u == 0:
                        pe.wait_ge(qk_loaded[heads - 1], 96)
                    scores(heads - 1, heads - 1, u)

            def group(g, last):
                for j in range(GROUP):
                    h = g * GROUP + j
                    pe.wait_ge(v_loaded[j % V_BUFS], (g * (GROUP // V_BUFS) + j // V_BUFS + 1) * 32)
                    for s in range(NS):
                        if (at := ahead(g, j, s, LEAD, last)) is not None:
                            scores_t(*at)
                        for heads, u in BESIDE[s]:
                            if last and j + heads >= GROUP:
                                continue
                            par = (j + heads) % QK_BUFS
                            if u == 0:
                                pe.wait_ge(qk_loaded[par], (g + (j + heads) // QK_BUFS + 1) * 96)
                            scores(h + heads, par, u)
                        if s >= NS - TC and not (last and j + 1 >= GROUP):
                            turn_max(h + 1, s - (NS - TC))
                        product_v(h, j % V_BUFS, s)

            with pe.Fori(0, NH // GROUP - 1) as g:
                group(g, False)
            group(NH // GROUP - 1, True)


def project_and_feed_forward(nc, x_t, xn_lo_scratch, gate_p, up_p, gate_up_s, down_p, down_s, xn_hi, xn_lo, wo_sb,
                             acc, out_t):
    CN = 2 * P
    CHUNKS = MLP // CN
    PAIR = 2
    ROUND = PAIR * TC
    NB = 8
    REP = P // NB
    GELU_A = 0.044715
    GELU_B = 0.7978845608028654
    CODE_SCALE = float(2 ** 14)
    with ExitStack() as ctx:
        acc = acc[:, :].rearrange("p (k t) -> p k t", k=KT)

        def sb(name, shape, dt):
            return ctx.enter_context(nc.sbuf_tensor(name, shape, dt))

        def sem(name):
            return ctx.enter_context(nc.semaphore(name))

        packed = [sb("packed", [P, 3, W], I32)[:, :, :], wo_sb[:, 0:3, :].bitcast(I32)]
        scales = [sb(f"scales{i}", [P, 2, W], F32) for i in range(2)]
        down_scales = [sb("down_scales", [P, W], F32)[:, :], wo_sb[:, 3, :]]
        high = sb("high", [P, W], I32)
        pair = sb("pair", [P, W], I32)
        magnitude = sb("magnitude", [P, W], I32)
        weight = sb("weight", [P, 2, W], F32)
        w_hi = [sb(f"w_hi{i}", [P, 3, 2, W], F32R) for i in range(2)]
        w_lo = [sb(f"w_lo{i}", [P, 3, 2, W], F32R) for i in range(2)]
        gate = sb("gate", [P, 2, W], F32)
        poly = sb("poly", [P, 2, W], F32)
        inter = sb("inter", [P, 2, W], F32)
        i_hi = sb("i_hi", [P, 2, 2, W], F32R)
        i_lo = sb("i_lo", [P, 2, 2, W], F32R)
        p_gate = ctx.enter_context(nc.psum_tensor("p_gate", [P, 2, W], F32))
        p_up = ctx.enter_context(nc.psum_tensor("p_up", [P, 2, W], F32))
        p_out = ctx.enter_context(nc.psum_tensor("p_out", [P, KT, W], F32))

        xt_slots = [gate, poly, inter, scales[1]]

        def xt_slot(tc, half):
            return xt_slots[2 * (tc % 2) + half][:, :, :]

        def wo_banks(tc, half):
            return p_out[:, 2 * half:2 * half + 2, :] if tc % 2 else (p_gate, p_up)[half][:, :, :]

        xt_loaded = [sem(f"xt_loaded{tc}") for tc in range(TC)]
        xn_lo_loaded = sem("xn_lo_loaded")
        wo_projected = sem("wo_projected")
        wo_added = sem("wo_added")
        loaded = [sem(f"ffn_loaded{i}") for i in range(2)]
        unpacked = sem("unpacked")
        weight_hi = sem("weight_hi")
        weight_lo = sem("weight_lo")
        gate_done = sem("gate_done")
        up_done = sem("up_done")
        down_done = sem("down_done")
        gate_out = sem("gate_out")
        poly_done = sem("poly_done")
        pool_turns = sem("pool_turns")
        tanh_done = sem("tanh_done")
        gelu_done = sem("gelu_done")
        inter_done = sem("inter_done")
        i_hi_done = sem("i_hi_done")
        i_lo_done = sem("i_lo_done")
        added = sem("added")
        out_stored = sem("out_stored")
        block = ctx.enter_context(nc.Block())

        def load_chunk(sp, c, par):
            cols = bass.ds(c * CN, CN)
            for m, pk in enumerate((gate_p, up_p)):
                sp.dma_start(packed[par][:, m, :].rearrange("p (k n) -> p k n", k=2),
                             pk[:, cols].rearrange("(k p) n -> p k n", p=P)).then_inc(loaded[par], 16)
            sp.dma_start(packed[par][:, 2, :], down_p[bass.ds(c * P, P), :]).then_inc(loaded[par], 16)
            for b in range(NB):
                rows = slice(b * REP, (b + 1) * REP)
                sp.dma_start(scales[par][rows, :, :].rearrange("p m (k n) -> p m k n", k=2),
                             gate_up_s[:, :, b, cols].partition_broadcast(REP)).then_inc(loaded[par], 16)
                sp.dma_start(down_scales[par][rows, :], down_s[bass.ds(c * NB + b, 1), :].rearrange("a h -> (a h)")
                             .partition_broadcast(REP)).then_inc(loaded[par], 16)
        LOADED = 16 * (3 + 2 * NB)

        @block.sync
        def _(sp):
            load_chunk(sp, 0, 0)
            for tc in range(TC):
                for half in range(2):
                    if tc >= 2:
                        sp.wait_ge(wo_added, 2 * (tc - 2) + half + 1)
                    rows = slice(half * 2 * P, (half + 1) * 2 * P)
                    sp.dma_start(xt_slot(tc, half), x_t[rows, tc * W:(tc + 1) * W]
                                 .rearrange("(k p) t -> p k t", p=P)).then_inc(xt_loaded[tc], 16)
                if tc == 1:
                    sp.dma_start(xn_lo[:, :, :].bitcast(F32), xn_lo_scratch).then_inc(xn_lo_loaded, 16)
            sp.wait_ge(wo_projected, TC)
            sp.wait_ge(wo_added, 2 * TC)
            load_chunk(sp, 1, 1)

            def round_(i, last):
                for half in range(PAIR):
                    c = PAIR * i + half
                    if not last:
                        sp.wait_ge(weight_lo, 3 * (c + 1))
                        load_chunk(sp, c + 2, half)

            with sp.Fori(0, CHUNKS // PAIR - 1) as i:
                round_(i, False)
            for tc in range(TC):
                sp.wait_ge(added, (CHUNKS - 1) * TC + tc + 2)
                sp.dma_start(out_t[:, tc * W:(tc + 1) * W].rearrange("(k p) t -> p k t", p=P),
                             acc[:, :, tc * W:(tc + 1) * W]).then_inc(out_stored, 16)
            sp.wait_ge(out_stored, 16 * TC)

        def steps(eng, body):
            with eng.Fori(0, CHUNKS // PAIR - 1) as i:
                for j in range(ROUND):
                    body(i, j, False, j % TC == 3)
            for j in range(ROUND):
                body(CHUNKS // PAIR - 1, j, j == ROUND - 1, j % TC == 3 or j >= TC)

        def next_chunk(i, j):
            return PAIR * i + j // TC + 1, (j // TC + 1) % 2, i + 1 + j // TC

        @block.scalar
        def _(act):
            def hi_weights(c, par, m, first=False):
                act.wait_ge(unpacked, 7 * (3 * c + m + 1))
                if not first:
                    act.wait_ge(*((up_done, (c - 1) * TC + 1) if m < 2 else (down_done, (c - 1) * TC + 2)))
                nc.scalar.activation(w_hi[par][:, m, :, :], weight[:, :, :], ACT.Copy,
                                     scale=CODE_SCALE).then_inc(weight_hi, 1)

            def elementwise(n, buf):
                act.wait_ge(gate_done, n + 1)
                act.wait_ge(gelu_done, n + 1)
                nc.scalar.activation(gate[:, :, :], p_gate[:, :, :], ACT.Copy).then_inc(gate_out, 1)
                nc.scalar.activation(poly[:, :, :], p_gate[:, :, :], ACT.Square).then_inc(gate_out, 1)
                act.wait_ge(poly_done, 2 * n + 2)
                act.wait_ge(i_lo_done, n + 1)
                nc.scalar.activation(inter[:, :, :], poly[:, :, :], ACT.Tanh, scale=GELU_B).then_inc(tanh_done, 1)
                act.wait_ge(inter_done, n + 2)
                act.wait_ge(down_done, n + 1)
                nc.scalar.activation(i_hi[:, buf, :, :], inter[:, :, :], ACT.Copy).then_inc(i_hi_done, 1)

            def body(i, j, final, no_weights):
                if not no_weights:
                    c, par, _ = next_chunk(i, j)
                    hi_weights(c, par, j % TC)
                if not final:
                    elementwise(ROUND * i + j + 1, (j + 1) % 2)

            act.sem_inc(gate_out, 2)
            for m in range(3):
                hi_weights(0, 0, m, first=True)
            act.wait_ge(wo_added, 2 * TC)
            elementwise(0, 0)
            steps(act, body)

        @block.gpsimd
        def _(pool):
            def elementwise(n):
                pool.wait_ge(gate_out, 2 * n + 4)
                pool.sem_inc(pool_turns, 1)
                nc.gpsimd.tensor_scalar(poly[:, :, :], poly[:, :, :], GELU_A, 1.0, ALU.mult,
                                        ALU.add).then_inc(poly_done, 1)
                pool.wait_ge(poly_done, 2 * n + 1)
                nc.gpsimd.tensor_tensor(poly[:, :, :], poly[:, :, :], gate[:, :, :], ALU.mult).then_inc(poly_done, 1)

            def body(i, j, final, no_weights):
                if not final:
                    elementwise(ROUND * i + j + 1)

            elementwise(0)
            steps(pool, body)

        @block.vector
        def _(dve):
            def unpack(c, par, m, loads, first=False):
                k = 3 * c + m
                pk = packed[par][:, m, :]

                def own(step):
                    dve.wait_ge(unpacked, 7 * k + step)
                dve.wait_ge(loaded[par], LOADED * loads)
                if not (first and m == 0):
                    own(0)
                    dve.wait_ge(weight_lo, k)
                nc.vector.tensor_scalar(high[:, :], pk, 0xF0, 12, ALU.bitwise_and,
                                        ALU.logical_shift_left).then_inc(unpacked, 1)
                nc.vector.tensor_scalar(pair[:, :], pk, 0x0F, None, ALU.bitwise_and).then_inc(unpacked, 1)
                own(2)
                nc.vector.tensor_tensor(pair[:, :], pair[:, :], high[:, :], ALU.bitwise_or).then_inc(unpacked, 1)
                own(3)
                nc.vector.tensor_scalar(magnitude[:, :], pair[:, :], 0x00070007, 9, ALU.bitwise_and,
                                        ALU.logical_shift_left).then_inc(unpacked, 1)
                nc.vector.tensor_scalar(high[:, :], pair[:, :], 0x00080008, 12, ALU.bitwise_and,
                                        ALU.logical_shift_left).then_inc(unpacked, 1)
                own(5)
                nc.vector.tensor_tensor(magnitude[:, :], magnitude[:, :], high[:, :],
                                        ALU.bitwise_or).then_inc(unpacked, 1)
                own(6)
                codes = magnitude[:, :].bitcast(F16).rearrange("p (n a) -> p a n", a=2)
                sc = (scales[par][:, m, :] if m < 2 else down_scales[par]).unsqueeze(1).broadcast_to([P, 2, W])
                nc.vector.tensor_tensor(weight[:, :, :], codes, sc, ALU.mult).then_inc(unpacked, 1)

            def lo_weights(c, par, m):
                dve.wait_ge(weight_hi, 3 * c + m + 1)
                nc.vector.scalar_tensor_tensor(w_lo[par][:, m, :, :], weight[:, :, :], CODE_SCALE,
                                               w_hi[par][:, m, :, :].bitcast(F32), ALU.mult,
                                               ALU.subtract).then_inc(weight_lo, 1)

            def elementwise(n, buf):
                dve.wait_ge(tanh_done, n + 1)
                nc.vector.scalar_tensor_tensor(inter[:, :, :], inter[:, :, :], 1.0, gate[:, :, :],
                                               ALU.add, ALU.mult).then_inc(gelu_done, 1)
                dve.wait_ge(gelu_done, n + 2)
                dve.wait_ge(up_done, n + 2)
                nc.vector.scalar_tensor_tensor(inter[:, :, :], inter[:, :, :], 0.5, p_up[:, :, :],
                                               ALU.mult, ALU.mult).then_inc(inter_done, 1)
                dve.wait_ge(i_hi_done, n + 1)
                nc.vector.tensor_tensor(i_lo[:, buf, :, :], inter[:, :, :], i_hi[:, buf, :, :].bitcast(F32),
                                        ALU.subtract).then_inc(i_lo_done, 1)

            def body(i, j, final, no_weights):
                n = ROUND * i + j
                if not no_weights:
                    c, par, loads = next_chunk(i, j)
                    unpack(c, par, j % TC, loads)
                    lo_weights(c, par, j % TC)
                if not final:
                    elementwise(n + 1, (j + 1) % 2)
                dve.wait_ge(down_done, n + 3)
                here = acc[:, :, (j % TC) * W:(j % TC + 1) * W]
                nc.vector.tensor_tensor(here, here, p_out[:, :, :], ALU.add).then_inc(added, 1)

            dve.sem_inc(gelu_done, 1)
            dve.sem_inc(i_lo_done, 1)
            dve.sem_inc(inter_done, 1)
            dve.sem_inc(added, 1)
            for tc in range(TC):
                if tc < 3:
                    unpack(0, 0, tc, 1, first=True)
                    lo_weights(0, 0, tc)
                dve.wait_ge(xt_loaded[tc], 32)
                dve.wait_ge(wo_projected, tc + 1)
                for half in range(2):
                    nc.vector.tensor_tensor(acc[:, 2 * half:2 * half + 2, tc * W:(tc + 1) * W], xt_slot(tc, half),
                                            wo_banks(tc, half), ALU.add).then_inc(wo_added, 1)
            elementwise(0, 0)
            steps(dve, body)

        @block.tensor
        def _(pe):
            def gate_and_up(i, j, n):
                par = j // TC % 2
                tokens = slice((j % TC) * W, (j % TC + 1) * W)
                for m, bank, free, done in ((0, p_gate, gate_out, gate_done), (1, p_up, inter_done, up_done)):
                    if j % TC == 0:
                        pe.wait_ge(weight_lo, 3 * (PAIR * i + j // TC) + m + 1)
                    pe.wait_ge(free, 2 * n + 2 if m == 0 else n + 1)
                    for nt in range(2):
                        for kt in range(KT):
                            rows = slice((kt % 2) * CN + nt * P, (kt % 2) * CN + (nt + 1) * P)
                            last = mm3(nc, bank[:, nt, :], w_hi[par][:, m, kt // 2, rows],
                                       w_lo[par][:, m, kt // 2, rows], xn_hi[:, kt, tokens], xn_lo[:, kt, tokens],
                                       kt == 0, kt == KT - 1)
                    last.then_inc(done, 1)

            def down(i, j, n):
                par = j // TC % 2
                if j % TC == 0:
                    pe.wait_ge(weight_lo, 3 * (PAIR * i + j // TC) + 3)
                pe.wait_ge(i_lo_done, n + 2)
                pe.wait_ge(added, n + 1)
                for ot in range(KT):
                    for nt in range(2):
                        last = mm3(nc, p_out[:, ot, :], w_hi[par][:, 2, nt, ot * P:(ot + 1) * P],
                                   w_lo[par][:, 2, nt, ot * P:(ot + 1) * P], i_hi[:, j % 2, nt, :],
                                   i_lo[:, j % 2, nt, :], nt == 0, nt == 1)
                last.then_inc(down_done, 1)

            def body(i, j, final, no_weights):
                n = ROUND * i + j
                if not final:
                    ni, nj = (i + 1, 0) if j == ROUND - 1 else (i, j + 1)
                    gate_and_up(ni, nj, n + 1)
                down(i, j, n)

            pe.sem_inc(up_done, 1)
            pe.sem_inc(down_done, 2)
            for tc in range(TC):
                for half in range(2):
                    if tc >= 2:
                        pe.wait_ge(wo_added, 2 * (tc - 2) + half + 1)
                    for i in range(2):
                        ot = 2 * half + i
                        for g in range(KT):
                            last = nc.tensor.matmul(wo_banks(tc, half)[:, i, :], wo_sb[:, g, ot * P:(ot + 1) * P],
                                                    acc[:, g, tc * W:(tc + 1) * W], start=g == 0, stop=g == KT - 1)
                last.then_inc(wo_projected, 1)
            pe.wait_ge(xn_lo_loaded, 16)
            pe.wait_ge(wo_added, 2 * (TC - 1))
            gate_and_up(0, 0, 0)
            pe.wait_ge(wo_added, 2 * TC)
            steps(pe, body)


def layer(nc, x, x_t, wqkv_t, wo_t, gate_p, up_p, gate_up_s, down_p, down_s, out_t):
    qk_scratch = nc.dram_tensor("qk_scratch", (2, 2, H, S), F32).ap()
    v_scratch = nc.dram_tensor("v_scratch", (S, 2 * NH, D), F32).ap()
    sum_scratch = nc.dram_tensor("sum_scratch", (NH, S), F32).ap()
    rsum_scratch = nc.dram_tensor("rsum_scratch", (NH, S), F32).ap()
    xn_lo_scratch = nc.dram_tensor("xn_lo_scratch", (P, KT, S), F32).ap()
    with nc.sbuf_tensor("xn_hi", [P, KT, S], F32R) as xn_hi:
        with nc.sbuf_tensor("xn_lo_made", [P, KT, S], F32R) as xn_lo:
            norm_and_project(nc, x, wqkv_t, qk_scratch, v_scratch, xn_lo_scratch, xn_hi, xn_lo)
        with (nc.sbuf_tensor("acc", [P, KT * S], F32) as acc,
              nc.sbuf_tensor("wo_sb", [P, KT, H], F32) as wo_sb):
            attention(nc, qk_scratch, v_scratch, sum_scratch, rsum_scratch, wo_t, wo_sb, acc)
            with nc.sbuf_tensor("xn_lo", [P, KT, S], F32R) as xn_lo:
                project_and_feed_forward(nc, x_t, xn_lo_scratch, gate_p, up_p, gate_up_s, down_p, down_s,
                                         xn_hi, xn_lo, wo_sb, acc, out_t)


def kernel(**inputs):
    import numpy as _np
    import concourse.bacc as _bacc
    from concourse import mybir as _mybir
    from concourse.bass_utils import run_bass_kernel_spmd as _run

    a = {k[3:]: _np.asarray(v) for k, v in inputs.items()}
    x = a["attn_hidden_states"].reshape(S, H)

    def by_tiles(w):
        return w.reshape(MLP // (2 * P), P, 2, -1).transpose(3, 0, 2, 1).reshape(w.shape[1], MLP)

    laid = {
        "x": x,
        "x_t": x.T,
        "wqkv_t": a["attn_w_qkv"].T.reshape(H // 2, 2, 3 * H).transpose(1, 0, 2).reshape(H, 3 * H),
        "wo_t": a["attn_w_o"].T,
        "gate_p": by_tiles(a["ffn_gate_W_packed"]),
        "up_p": by_tiles(a["ffn_up_W_packed"]),
        "gate_up_s": _np.stack([by_tiles(a["ffn_gate_scales"]), by_tiles(a["ffn_up_scales"])])
        .reshape(2, 2, H // 64, MLP),
        "down_p": a["ffn_down_W_packed"].T,
        "down_s": a["ffn_down_scales"].T,
    }
    nc = _bacc.Bacc("TRN2", target_bir_lowering=False, num_devices=1)
    arrays, args = {}, []
    for name, v in laid.items():
        v = _np.ascontiguousarray(v)
        arrays[f"in_{name}"] = v
        args.append(nc.dram_tensor(f"in_{name}", v.shape, _mybir.dt.from_np(v.dtype), kind="ExternalInput").ap())
    args.append(nc.dram_tensor("out_t", (H, S), _mybir.dt.float32, kind="ExternalOutput").ap())
    layer(nc, *args)
    r = _run(nc, [arrays], core_ids=[0])
    return _np.ascontiguousarray(r.results[0]["out_t"].T).reshape(1, S, H)
```
